# Optimizing a Trainium2 kernel written in Bass

```python
import numpy as np
import jax
import jax.numpy as jnp

def _softmax(x, axis=-1):
    return jax.nn.softmax(x, axis=axis)
def _gelu(x):
    return jax.nn.gelu(x, approximate=True)
def _silu(x):
    return jax.nn.silu(x)
def _sigmoid(x):
    return jax.nn.sigmoid(x)
def _layernorm(x, axis=-1, eps=1e-5):
    m = jnp.mean(x, axis=axis, keepdims=True)
    v = jnp.var(x, axis=axis, keepdims=True)
    return (x - m) / jnp.sqrt(v + eps)
def _scatter_add(tgt, idx, src, axis=0):
    return tgt.at[idx].add(src)
def _segment_sum(src, seg, n):
    return jax.ops.segment_sum(src, seg, n)

kernel_name = 'mk_conv_seq_d1_conv_nchw512_a3f8e4'

def setup_inputs(seed: int = 0):
    np.random.seed(seed)
    _w = jnp.asarray
    def _rec_inputs():
        import jax
        import jax.numpy as jnp
        _gk = jax.random.key(seed)
        x = -9.26e-05 + 0.9999 * jax.random.normal(jax.random.fold_in(_gk, 1), (8, 512, 96, 96), jnp.float32)
        return x
    x = _rec_inputs()
    def _L0_conv_setup():
        import jax, jax.numpy as jnp
        import numpy as np
        NEG_INF = -jnp.inf
        key = jax.random.key(seed)
        ks = jax.random.split(key, 8)
        B, C, H, W = (8, 512, 96, 96)
        IC = max(1, C // 8)
        s = 1.0 / np.sqrt(C)
        x = jax.random.normal(ks[0], (B, C, H, W), dtype=jnp.float32)
        Wq = jax.random.normal(ks[1], (IC, C), dtype=jnp.float32) * s
        bq = jax.random.normal(ks[2], (IC,), dtype=jnp.float32) * s
        Wk = jax.random.normal(ks[3], (IC, C), dtype=jnp.float32) * s
        bk = jax.random.normal(ks[4], (IC,), dtype=jnp.float32) * s
        Wv = jax.random.normal(ks[5], (C, C), dtype=jnp.float32) * s
        bv = jax.random.normal(ks[6], (C,), dtype=jnp.float32) * s
        gamma = jnp.full((1,), 0.5, dtype=jnp.float32)
        return {'x': x, 'Wq': Wq, 'bq': bq, 'Wk': Wk, 'bk': bk, 'Wv': Wv, 'bv': bv, 'gamma': gamma}
    _L0_conv_all = _L0_conv_setup()
    _L0_conv_in = {k: v for k, v in _L0_conv_all.items() if k in ('Wq', 'bq', 'Wk', 'bk', 'Wv', 'bv', 'gamma', )}
    del _L0_conv_all

    return {
        "x": x,
        "L0_conv_Wq": _L0_conv_in["Wq"],
        "L0_conv_bq": _L0_conv_in["bq"],
        "L0_conv_Wk": _L0_conv_in["Wk"],
        "L0_conv_bk": _L0_conv_in["bk"],
        "L0_conv_Wv": _L0_conv_in["Wv"],
        "L0_conv_bv": _L0_conv_in["bv"],
        "L0_conv_gamma": _L0_conv_in["gamma"],
    }

def reference(x, L0_conv_Wq, L0_conv_bq, L0_conv_Wk, L0_conv_bk, L0_conv_Wv, L0_conv_bv, L0_conv_gamma):
    import jax
    import jax.numpy as jnp
    def _L0_conv_ref(x, Wq, bq, Wk, bk, Wv, bv, gamma):
        import jax, jax.numpy as jnp
        import numpy as np
        NEG_INF = -jnp.inf
        B, C, H, W = x.shape
        q = jnp.einsum('oc,bchw->bohw', Wq, x) + bq[None, :, None, None]
        k = jnp.einsum('oc,bchw->bohw', Wk, x) + bk[None, :, None, None]
        v = jnp.einsum('oc,bchw->bohw', Wv, x) + bv[None, :, None, None]
        e_h = jnp.einsum('bchw,bcgw->bhwg', q, k)
        eye = jnp.eye(H, dtype=bool)[:, None, :]
        e_h = jnp.where(eye[None], NEG_INF, e_h)
        e_w = jnp.einsum('bchw,bchv->bhwv', q, k)
        attn = jax.nn.softmax(jnp.concatenate([e_h, e_w], axis=-1), axis=-1)
        a_h = attn[..., :H]
        a_w = attn[..., H:]
        out_h = jnp.einsum('bcgw,bhwg->bchw', v, a_h)
        out_w = jnp.einsum('bchv,bhwv->bchw', v, a_w)
        return gamma[0] * (out_h + out_w) + x

    def _gn(v, G=32, eps=1e-5):
        B_, C_, H_, W_ = v.shape
        g = v.reshape(B_, G, C_ // G, H_, W_)
        m = jnp.mean(g, axis=(2, 3, 4), keepdims=True)
        s = jnp.var(g, axis=(2, 3, 4), keepdims=True)
        return ((g - m) / jnp.sqrt(s + eps)).reshape(v.shape)

    def _ln_c(v, eps=1e-6):
        m = jnp.mean(v, axis=1, keepdims=True)
        s = jnp.var(v, axis=1, keepdims=True)
        return (v - m) / jnp.sqrt(s + eps)

    def _ln_t(v, eps=1e-5):
        m = jnp.mean(v, axis=-1, keepdims=True)
        s = jnp.var(v, axis=-1, keepdims=True)
        return (v - m) / jnp.sqrt(s + eps)

    def _to_tokens(v):
        B_, C_, H_, W_ = v.shape
        return v.reshape(B_, C_, H_ * W_).transpose(0, 2, 1)
    def _from_tokens(t, like):
        B_, C_, H_, W_ = like.shape
        return t.transpose(0, 2, 1).reshape(B_, C_, H_, W_)

    x = _L0_conv_ref(x, L0_conv_Wq, L0_conv_bq, L0_conv_Wk, L0_conv_bk, L0_conv_Wv, L0_conv_bv, L0_conv_gamma)
    return x


_drawn_inputs = setup_inputs


def setup_inputs(seed=0):
    import zlib

    import numpy as np

    out = dict(_drawn_inputs(seed))
    spreads = {}
    factors = {'L0_conv_bk': 8.0, 'L0_conv_bv': 2.693}
    for name, (base, spread) in spreads.items():
        noise = np.random.default_rng([zlib.crc32(name.encode()), seed]).standard_normal(out[name].shape)
        drawn = base * np.exp(spread * noise) if base else spread * noise
        out[name] = jnp.asarray(drawn.astype(out[name].dtype))
    for name, factor in factors.items():
        out[name] = (out[name] * factor).astype(out[name].dtype)
    return out
```

```python
from contextlib import ExitStack

import numpy as np
import concourse.bass as bass
from concourse import mybir

F32 = mybir.dt.float32
F32R = mybir.dt.float32r
ALU = mybir.AluOpType
ACT = mybir.ActivationFunctionType
AX_X = mybir.AxisListType.X

P = 128
MASKED = -3.0e38
FROM = 1
BANK = 512


def build_program(nc, x, wqk_t, bias_q, bias_k, wv_t, bv, gamma, ident, diag, out):
    B, C, H, W = x.shape
    x_t = nc.dram_tensor("x_t", (B, H, W, C), F32).ap()
    row_probs = nc.dram_tensor("row_probs", (B, W, H, W), F32).ap()
    col_probs = nc.dram_tensor("col_probs", (B, H, W, H), F32).ap()
    attention_weights(nc, x, wqk_t, bias_q, bias_k, ident, diag, x_t, row_probs, col_probs)
    attend_and_project(nc, x, wv_t, bv, gamma, ident, x_t, row_probs, col_probs, out)


def attention_weights(nc, x, wqk_t, bias_q, bias_k, ident_d, diag_d, x_t, row_probs, col_probs):
    B, C, H, W = x.shape
    KT = C // P
    IC = wqk_t.shape[1] // 2
    R = 4
    BP = R * W
    SLOTS = 4
    BODIES = H // (R * SLOTS)
    NB = H // R
    HALF = BODIES // 2
    CH = H // (HALF * SLOTS)
    NCH = H // CH
    PER = CH // R
    assert H == W and CH * NCH == H and HALF * 2 == BODIES

    with ExitStack() as ctx:
        def sb(name, shape, dt=F32):
            return ctx.enter_context(nc.sbuf_tensor(name, shape, dt))

        counted = []

        def sem(name):
            counted.append(ctx.enter_context(nc.semaphore(name)))
            return counted[-1]

        x_in = [sb(f"x_in{k}", [P, KT, BP]) for k in range(SLOTS)]
        xt_out = [sb(f"xt_out{p}", [W, R, C]) for p in range(2)]
        wqk = sb("wqk", [P, KT, 2 * IC])
        bq = sb("bq", [P, 1])
        bk = sb("bk", [P, 1])
        ident = sb("ident", [P, P])
        diag = sb("diag", [H, H])
        q_all = sb("q_all", [IC, H, W])
        k_all = sb("k_all", [IC, H, W])
        q_rows = [sb(f"q_rows{p}", [IC, R, W]) for p in range(2)]
        q_cols = [sb(f"q_cols{p}", [IC, R, H]) for p in range(2)]
        e_row = sb("e_row", [W, H, W])
        e_col = sb("e_col", [H, W, H])
        max_row = sb("max_row", [W, H])
        max_col = sb("max_col", [H, W])
        sum_row = sb("sum_row", [W, H])
        sum_col = sb("sum_col", [H, W])
        p_row_in = sb("p_row_in", [W, CH, W])
        p_col_in = sb("p_col_in", [H, CH, H])
        p_row_out = sb("p_row_out", [W, CH, W])
        p_col_out = sb("p_col_out", [H, CH, H])

        ps = ctx.enter_context(nc.psum_tensor("ps_a", [P, 8, BANK], F32))

        passed = ctx.enter_context(nc.semaphore("passed"))
        consts_in = ctx.enter_context(nc.semaphore("consts_in"))
        x_loaded = [sem(f"x_loaded{k}") for k in range(SLOTS)]
        qk_done = [sem(f"qk_done{k}") for k in range(SLOTS)]
        q_kept = [sem(f"q_kept{p}") for p in range(2)]
        k_kept = [sem(f"k_kept{p}") for p in range(2)]
        xt_turned = [sem(f"xt_turned{p}") for p in range(2)]
        xt_kept = [sem(f"xt_kept{p}") for p in range(2)]
        xt_stored = [sem(f"xt_stored{p}") for p in range(2)]
        q_rows_laid = [sem(f"q_rows_laid{p}") for p in range(2)]
        q_cols_laid = [sem(f"q_cols_laid{p}") for p in range(2)]
        e_row_mm = [sem(f"e_row_mm{p}") for p in range(2)]
        e_col_mm = [sem(f"e_col_mm{p}") for p in range(2)]
        e_row_kept = [sem(f"e_row_kept{p}") for p in range(2)]
        e_col_kept = [sem(f"e_col_kept{p}") for p in range(2)]
        max_done = sem("max_done")
        stat_turned = sem("stat_turned")
        joint_done = sem("joint_done")
        total_done = sem("total_done")
        inv_done = sem("inv_done")
        shifted = sem("shifted")
        exp_done = sem("exp_done")
        sum_done = sem("sum_done")
        scaled_row = sem("scaled_row")
        scaled_col = sem("scaled_col")
        p_row_turned = [sem(f"p_row_turned{p}") for p in range(PER)]
        p_col_turned = [sem(f"p_col_turned{p}") for p in range(PER)]
        p_row_kept = [sem(f"p_row_kept{p}") for p in range(PER)]
        p_col_kept = [sem(f"p_col_kept{p}") for p in range(PER)]
        p_row_stored = sem("p_row_stored")
        p_col_stored = sem("p_col_stored")

        QK_BANK, XT_BANK, ROW_BANK, COL_BANK = 0, 2, 4, 6
        UP = NB // 2

        def apart(eng):
            eng.sem_inc(passed, 1)

        def loop(eng, n, body):
            with eng.Fori(0, n) as i:
                body(i)

        block = ctx.enter_context(nc.Block())

        @block.sync
        def _(sp):
            sp.dma_start(wqk[:, :, :], wqk_t.rearrange("(t p) o -> p t o", p=P)).then_inc(consts_in, 16)
            sp.dma_start(bq[:, :], bias_q).then_inc(consts_in, 16)
            sp.dma_start(bk[:, :], bias_k).then_inc(consts_in, 16)
            sp.dma_start(ident[:, :], ident_d).then_inc(consts_in, 16)
            sp.dma_start(diag[:, :], diag_d).then_inc(consts_in, 16)

            def image(b):
                def body(i):
                    for k in range(SLOTS):
                        sp.wait_ge(qk_done[k], FROM + b * BODIES + i)
                        sp.dma_start(
                            x_in[k][:, :, :],
                            x[bass.ds(b, 1), :, bass.ds(i * (SLOTS * R) + k * R, R), :].rearrange(
                                "b (t p) h w -> p (b t) (h w)", p=P)).then_inc(x_loaded[k], 16)
                loop(sp, BODIES, body)
            loop(sp, B, image)

        @block.tensor
        def _(pe):
            pe.wait_ge(consts_in, 5 * 16)

            def x_block(b, i, k):
                n = b * NB + i * SLOTS + k
                bank = k % 2
                used = (b * BODIES + i) * (SLOTS // 2) + k // 2
                pe.wait_ge(x_loaded[k], FROM + (b * BODIES + i + 1) * 16)
                for half in range(2):
                    for p in range(2):
                        r = 2 * half + p
                        pe.wait_ge(xt_kept[p], FROM + n * (R // 2) + half)
                        for t in range(KT):
                            mm = nc.tensor.transpose(ps[0:W, XT_BANK + p, t * P:(t + 1) * P],
                                                     x_in[k][:, t, r * W:(r + 1) * W], ident[:, :])
                        mm.then_inc(xt_turned[p], 1)
                    if half == 0:
                        pe.wait_ge(q_kept[bank], FROM + used)
                        pe.wait_ge(k_kept[bank], FROM + used)
                    for t in range(half * KT // 2, (half + 1) * KT // 2):
                        mm = nc.tensor.matmul(ps[:, QK_BANK + bank, 0:BP], wqk[:, t, :], x_in[k][:, t, :],
                                              start=(t == 0), stop=(t == KT - 1))
                mm.then_inc(qk_done[k], 1)

            def energies(b):
                for p in range(2):
                    pe.wait_ge(k_kept[p], FROM + (b + 1) * (NB // 2))
                apart(pe)

                def body(i):
                    for p in range(2):
                        at = b * UP + i
                        pe.wait_ge(q_rows_laid[p], FROM + at + 1)
                        pe.wait_ge(e_row_kept[p], FROM + at)
                        for r in range(R):
                            mm = nc.tensor.matmul(ps[0:W, ROW_BANK + p, r * W:(r + 1) * W],
                                                  q_rows[p][:, r, :],
                                                  k_all[:, bass.ds(i * (2 * R) + p * R + r, 1), :].rearrange(
                                                      "c a w -> c (a w)"), start=True, stop=True)
                        mm.then_inc(e_row_mm[p], 1)
                        pe.wait_ge(q_cols_laid[p], FROM + at + 1)
                        pe.wait_ge(e_col_kept[p], FROM + at)
                        for r in range(R):
                            mm = nc.tensor.matmul(ps[0:H, COL_BANK + p, r * H:(r + 1) * H],
                                                  q_cols[p][:, r, :],
                                                  k_all[:, :, bass.ds(i * (2 * R) + p * R + r, 1)].rearrange(
                                                      "c h a -> c (h a)"), start=True, stop=True)
                        mm.then_inc(e_col_mm[p], 1)
                loop(pe, UP, body)

            def turn_stats(row, col):
                nc.tensor.transpose(ps[0:H, ROW_BANK, 0:W], row[:, :], ident[0:W, 0:W]).then_inc(stat_turned, 1)
                nc.tensor.transpose(ps[0:W, COL_BANK, 0:H], col[:, :], ident[0:H, 0:H]).then_inc(stat_turned, 1)

            def turn_maxima(b):
                pe.wait_ge(max_done, FROM + (b + 1) * NB * 2)
                turn_stats(max_row, max_col)

            def turn_sums(b):
                pe.wait_ge(sum_done, FROM + (b + 1) * NCH * 2)
                turn_stats(sum_row, sum_col)

            def turn_probs(b, chunk):
                at = b * NCH + chunk
                pe.wait_ge(scaled_row, FROM + at + 1)
                for p in range(PER):
                    pe.wait_ge(p_row_kept[p], FROM + at)
                    for r in range(R):
                        mm = nc.tensor.transpose(
                            ps[0:W, ROW_BANK + p, r * W:(r + 1) * W],
                            p_row_in[:, p * R + r, :], ident[0:W, 0:W])
                    mm.then_inc(p_row_turned[p], 1)
                pe.wait_ge(scaled_col, FROM + at + 1)
                for p in range(PER):
                    pe.wait_ge(p_col_kept[p], FROM + at)
                    for r in range(R):
                        mm = nc.tensor.transpose(
                            ps[0:H, COL_BANK + p, r * H:(r + 1) * H],
                            p_col_in[:, p * R + r, :], ident[0:H, 0:H])
                    mm.then_inc(p_col_turned[p], 1)

            def drained(b):
                for p in range(PER):
                    pe.wait_ge(p_row_kept[p], FROM + (b + 1) * NCH)
                    pe.wait_ge(p_col_kept[p], FROM + (b + 1) * NCH)

            def first(i):
                for k in range(SLOTS):
                    x_block(0, i, k)
            loop(pe, BODIES, first)
            energies(0)
            turn_maxima(0)

            def image(c):
                b = c + 1
                def exps(i):
                    for k in range(SLOTS):
                        x_block(b, i, k)
                loop(pe, HALF, exps)
                turn_sums(c)
                pe.wait_ge(total_done, FROM + b * 2)
                apart(pe)

                def norms(i):
                    for k in range(SLOTS):
                        x_block(b, i + HALF, k)
                        turn_probs(c, i * SLOTS + k)
                loop(pe, HALF, norms)
                drained(c)
                energies(b)
                turn_maxima(b)
            if B > 1:
                loop(pe, B - 1, image)
            turn_sums(B - 1)
            pe.wait_ge(total_done, FROM + B * 2)

            def last(i):
                for k in range(SLOTS):
                    turn_probs(B - 1, i * SLOTS + k)
            loop(pe, HALF, last)

        @block.scalar
        def _(act):
            act.wait_ge(consts_in, 5 * 16)

            def x_block(b, i, k):
                n = b * NB + i * SLOTS + k
                slot = k % 2
                used = (b * BODIES + i) * (SLOTS // 2) + k // 2
                act.wait_ge(xt_stored[slot], FROM + used * 16)
                for r in range(0, R, 2):
                    act.wait_ge(xt_turned[0], FROM + n * (R // 2) + r // 2 + 1)
                    nc.scalar.activation(xt_out[slot][:, r, :], ps[0:W, XT_BANK, 0:C],
                                         ACT.Copy).then_inc(xt_kept[0], 1)
                act.wait_ge(qk_done[k], FROM + b * BODIES + i + 1)
                nc.scalar.activation(
                    q_all[:, bass.ds(i * (SLOTS * R) + k * R, R), :].rearrange("c h w -> c (h w)"),
                    ps[0:IC, QK_BANK + slot, 0:BP], ACT.Identity,
                    bias=bq[0:IC, 0:1], scale=1.0).then_inc(q_kept[slot], 1)
                act.wait_ge(xt_kept[0], FROM + (n + 1) * (R // 2))
                act.wait_ge(xt_kept[1], FROM + (n + 1) * (R // 2))
                act.dma_start(
                    x_t[bass.ds(b, 1), bass.ds(i * (SLOTS * R) + k * R, R), :, :].rearrange(
                        "b h w c -> w (b h) c"), xt_out[slot][:, :, :]).then_inc(xt_stored[slot], 16)

            def energies(b):
                def lay_rows(i, p):
                    act.wait_ge(e_row_mm[p], FROM + b * UP + i)
                    apart(act)
                    nc.scalar.activation(
                        q_rows[p][:, :, :].rearrange("c h w -> c (h w)"),
                        q_all[:, bass.ds(i * (2 * R) + p * R, R), :].rearrange("c h w -> c (h w)"),
                        ACT.Copy).then_inc(q_rows_laid[p], 1)

                def keep(i, p):
                    act.wait_ge(e_row_mm[p], FROM + b * UP + i + 1)
                    apart(act)
                    nc.scalar.activation(
                        e_row[:, bass.ds(i * (2 * R) + p * R, R), :].rearrange("w h v -> w (h v)"),
                        ps[0:W, ROW_BANK + p, 0:BP], ACT.Copy).then_inc(e_row_kept[p], 1)

                for p in range(2):
                    act.wait_ge(q_kept[p], FROM + (b + 1) * (NB // 2))
                lay_rows(0, 0)

                def body(i):
                    lay_rows(i, 1)
                    keep(i, 0)
                    lay_rows(i + 1, 0)
                    keep(i, 1)
                loop(act, UP - 1, body)
                lay_rows(UP - 1, 1)
                keep(UP - 1, 0)
                keep(UP - 1, 1)

            def exps(b, chunk):
                at = b * NCH + chunk
                for j, e in enumerate((e_row, e_col)):
                    act.wait_ge(shifted, FROM + at * 2 + j + 1)
                    apart(act)
                    part = e[:, bass.ds(chunk * CH, CH), :].rearrange("a b c -> a (b c)")
                    nc.scalar.activation(part, part, ACT.Exp).then_inc(exp_done, 1)

            def keep_probs(b, chunk):
                at = b * NCH + chunk
                act.wait_ge(p_row_stored, FROM + at * 16)
                for p in range(PER):
                    act.wait_ge(p_row_turned[p], FROM + at + 1)
                    nc.scalar.activation(
                        p_row_out[:, p * R:(p + 1) * R, :].rearrange("v h w -> v (h w)"),
                        ps[0:W, ROW_BANK + p, 0:BP], ACT.Copy).then_inc(p_row_kept[p], 1)
                for p in range(PER):
                    act.wait_ge(p_row_kept[p], FROM + at + 1)
                apart(act)
                act.dma_start(
                    row_probs[bass.ds(b, 1), :, bass.ds(chunk * CH, CH), :].rearrange("b v h w -> v (b h) w"),
                    p_row_out[:, :, :]).then_inc(p_row_stored, 16)
                for p in range(PER):
                    act.wait_ge(p_col_kept[p], FROM + at + 1)
                apart(act)
                act.dma_start(
                    col_probs[bass.ds(b, 1), :, bass.ds(chunk * CH, CH), :].rearrange("b g w h -> g (b w) h"),
                    p_col_out[:, :, :]).then_inc(p_col_stored, 16)

            def first(i):
                for k in range(SLOTS):
                    x_block(0, i, k)
            loop(act, BODIES, first)
            energies(0)

            def image(c):
                b = c + 1
                for p in range(2):
                    act.wait_ge(e_row_mm[p], FROM + b * UP)
                    act.wait_ge(e_col_mm[p], FROM + b * UP)
                apart(act)

                def exp_body(i):
                    for k in range(SLOTS):
                        x_block(b, i, k)
                        exps(c, i * SLOTS + k)
                loop(act, HALF, exp_body)

                def norm_body(i):
                    for k in range(SLOTS):
                        x_block(b, i + HALF, k)
                        keep_probs(c, i * SLOTS + k)
                loop(act, HALF, norm_body)
                energies(b)
            if B > 1:
                loop(act, B - 1, image)

            def last_exps(i):
                for k in range(SLOTS):
                    exps(B - 1, i * SLOTS + k)
            loop(act, HALF, last_exps)

            def last_probs(i):
                for k in range(SLOTS):
                    keep_probs(B - 1, i * SLOTS + k)
            loop(act, HALF, last_probs)
            act.wait_ge(p_row_stored, FROM + B * NCH * 16)
            act.wait_ge(p_col_stored, FROM + B * NCH * 16)
            for p in range(2):
                act.wait_ge(xt_stored[p], FROM + B * NB // 2 * 16)

        @block.vector
        def _(dve):
            dve.wait_ge(consts_in, 5 * 16)

            def x_block(b, i, k):
                n = b * NB + i * SLOTS + k
                slot = k % 2
                used = (b * BODIES + i) * (SLOTS // 2) + k // 2
                dve.wait_ge(xt_stored[slot], FROM + used * 16)
                for r in range(1, R, 2):
                    dve.wait_ge(xt_turned[1], FROM + n * (R // 2) + r // 2 + 1)
                    nc.vector.tensor_copy(xt_out[slot][:, r, :],
                                          ps[0:W, XT_BANK + 1, 0:C]).then_inc(xt_kept[1], 1)
                dve.wait_ge(qk_done[k], FROM + b * BODIES + i + 1)
                nc.vector.tensor_scalar(
                    k_all[:, bass.ds(i * (SLOTS * R) + k * R, R), :].rearrange("c h w -> c (h w)"),
                    ps[IC:2 * IC, QK_BANK + slot, 0:BP], bk[IC:2 * IC, 0:1], None,
                    ALU.add).then_inc(k_kept[slot], 1)

            def energies(b):
                def body(i):
                    for p in range(2):
                        at = b * UP + i
                        first = i * (2 * R) + p * R
                        dve.wait_ge(e_col_mm[p], FROM + at + 1)
                        part = e_col[:, bass.ds(first, R), :]
                        nc.vector.tensor_tensor(
                            part, ps[0:H, COL_BANK + p, 0:BP].rearrange("h (w g) -> h w g", w=R),
                            diag[:, :].unsqueeze(1).to_broadcast([H, R, H]), ALU.add).then_inc(e_col_kept[p], 1)
                        dve.wait_ge(e_row_kept[p], FROM + at + 1)
                        nc.vector.tensor_reduce(max_row[:, bass.ds(first, R)], e_row[:, bass.ds(first, R), :],
                                                AX_X, ALU.max).then_inc(max_done, 1)
                        dve.wait_ge(e_col_kept[p], FROM + at + 1)
                        nc.vector.tensor_reduce(max_col[:, bass.ds(first, R)], part,
                                                AX_X, ALU.max).then_inc(max_done, 1)
                loop(dve, UP, body)

            def join_maxima(b):
                dve.wait_ge(stat_turned, FROM + b * 4 + 2)
                nc.vector.tensor_tensor(max_col[:, :], ps[0:H, ROW_BANK, 0:W], max_col[:, :],
                                        ALU.max).then_inc(joint_done, 1)
                nc.vector.tensor_tensor(max_row[:, :], ps[0:W, COL_BANK, 0:H], max_row[:, :],
                                        ALU.max).then_inc(joint_done, 1)

            def join_sums(b):
                dve.wait_ge(stat_turned, FROM + b * 4 + 4)
                nc.vector.tensor_tensor(sum_col[:, :], ps[0:H, ROW_BANK, 0:W], sum_col[:, :],
                                        ALU.add).then_inc(total_done, 1)
                nc.vector.tensor_tensor(sum_row[:, :], ps[0:W, COL_BANK, 0:H], sum_row[:, :],
                                        ALU.add).then_inc(total_done, 1)
                dve.wait_ge(total_done, FROM + b * 2 + 2)
                nc.vector.reciprocal(sum_row[:, :], sum_row[:, :]).then_inc(inv_done, 1)
                nc.vector.reciprocal(sum_col[:, :], sum_col[:, :]).then_inc(inv_done, 1)
                dve.wait_ge(inv_done, FROM + b * 2 + 2)
                apart(dve)

            def sums(b, chunk):
                at = b * NCH + chunk
                for j, (e, s) in enumerate(((e_row, sum_row), (e_col, sum_col))):
                    dve.wait_ge(exp_done, FROM + at * 2 + j + 1)
                    nc.vector.tensor_reduce(s[:, bass.ds(chunk * CH, CH)], e[:, bass.ds(chunk * CH, CH), :],
                                            AX_X, ALU.add).then_inc(sum_done, 1)

            def scale_cols(b, chunk):
                at = b * NCH + chunk
                for p in range(PER):
                    dve.wait_ge(p_col_turned[p], FROM + at)
                nc.vector.tensor_tensor(
                    p_col_in[:, :, :], e_col[:, bass.ds(chunk * CH, CH), :],
                    sum_col[:, bass.ds(chunk * CH, CH)].unsqueeze(2).to_broadcast([H, CH, H]),
                    ALU.mult).then_inc(scaled_col, 1)

            def keep_probs(b, chunk):
                at = b * NCH + chunk
                dve.wait_ge(p_col_stored, FROM + at * 16)
                for p in range(PER):
                    dve.wait_ge(p_col_turned[p], FROM + at + 1)
                    nc.vector.tensor_copy(
                        p_col_out[:, p * R:(p + 1) * R, :].rearrange("g w h -> g (w h)"),
                        ps[0:H, COL_BANK + p, 0:BP]).then_inc(p_col_kept[p], 1)

            def first(i):
                for k in range(SLOTS):
                    x_block(0, i, k)
            loop(dve, BODIES, first)
            energies(0)
            join_maxima(0)

            def image(c):
                b = c + 1
                for p in range(2):
                    dve.wait_ge(e_row_mm[p], FROM + b * UP)
                    dve.wait_ge(e_col_mm[p], FROM + b * UP)
                apart(dve)

                def exp_body(i):
                    for k in range(SLOTS):
                        x_block(b, i, k)
                        sums(c, i * SLOTS + k)
                loop(dve, HALF, exp_body)
                join_sums(c)

                def norm_body(i):
                    for k in range(SLOTS):
                        scale_cols(c, i * SLOTS + k)
                        x_block(b, i + HALF, k)
                        keep_probs(c, i * SLOTS + k)
                loop(dve, HALF, norm_body)
                energies(b)
                join_maxima(b)
            if B > 1:
                loop(dve, B - 1, image)

            def last_sums(i):
                for k in range(SLOTS):
                    sums(B - 1, i * SLOTS + k)
            loop(dve, HALF, last_sums)
            join_sums(B - 1)

            def last_probs(i):
                for k in range(SLOTS):
                    scale_cols(B - 1, i * SLOTS + k)
                    keep_probs(B - 1, i * SLOTS + k)
            loop(dve, HALF, last_probs)

        @block.gpsimd
        def _(pool):
            for s in counted:
                pool.sem_inc(s, FROM)

            def energies(b):
                for p in range(2):
                    pool.wait_ge(q_kept[p], FROM + (b + 1) * (NB // 2))
                apart(pool)

                def body(i):
                    for p in range(2):
                        at = b * UP + i
                        first = i * (2 * R) + p * R
                        pool.wait_ge(e_col_mm[p], FROM + at)
                        nc.gpsimd.tensor_copy(q_cols[p][:, :, :],
                                              q_all[:, :, bass.ds(first, R)].rearrange("c h w -> c w h"),
                                              ).then_inc(q_cols_laid[p], 1)
                loop(pool, UP, body)

            def shift(b):
                pool.wait_ge(joint_done, FROM + (b + 1) * 2)
                apart(pool)

                def body(i):
                    for k in range(SLOTS):
                        chunk = i * SLOTS + k
                        for e, m in ((e_row, max_row), (e_col, max_col)):
                            part = e[:, bass.ds(chunk * CH, CH), :]
                            nc.gpsimd.tensor_tensor(
                                part, part, m[:, bass.ds(chunk * CH, CH)].unsqueeze(2).to_broadcast([H, CH, H]),
                                ALU.subtract).then_inc(shifted, 1)
                loop(pool, HALF, body)

            def scale_rows(b):
                pool.wait_ge(inv_done, FROM + (b + 1) * 2)
                apart(pool)

                def body(i):
                    for k in range(SLOTS):
                        chunk = i * SLOTS + k
                        for p in range(PER):
                            pool.wait_ge(p_row_turned[p], FROM + b * NCH + chunk)
                        nc.gpsimd.tensor_tensor(
                            p_row_in[:, :, :], e_row[:, bass.ds(chunk * CH, CH), :],
                            sum_row[:, bass.ds(chunk * CH, CH)].unsqueeze(2).to_broadcast([W, CH, W]),
                            ALU.mult).then_inc(scaled_row, 1)
                loop(pool, HALF, body)

            def image(b):
                energies(b)
                shift(b)
                scale_rows(b)
            loop(pool, B, image)


def attend_and_project(nc, x, wv_t, bv_d, gamma_d, ident_d, x_t, row_probs, col_probs, out):
    B, C, H, W = x.shape
    CT = C // P
    R = 3
    UP = R * W
    NU = H // R
    PAIRS = NU // 2
    SLOTS = 4
    FOURS = NU // SLOTS
    assert H == W and NU % SLOTS == 0 and (SLOTS - 2) * R * C <= 4 * CT * UP

    with ExitStack() as ctx:
        def sb(name, shape, dt=F32):
            return ctx.enter_context(nc.sbuf_tensor(name, shape, dt))

        counted = []

        def sem(name):
            counted.append(ctx.enter_context(nc.semaphore(name)))
            return counted[-1]

        y = sb("y", [P, CT, H * W])
        probs = [sb(f"probs{p}", [H, R, W]) for p in range(SLOTS)]
        x_res = [sb(f"x_res{p}", [P, CT, UP]) for p in range(2)]
        parts = sb("parts", [P, 4 * CT * UP], F32R)

        def part(j):
            return parts[:, j * CT * UP:(j + 1) * CT * UP].rearrange("p (t n) -> p t n", t=CT)
        y_hi = [part(0), part(1)]
        y_lo = [part(2), part(3)]
        xt_in = [sb(f"xt_in{p}", [H, R, C])[:, :, :] for p in range(2)]
        xt_in += [parts[0:H, j * R * C:(j + 1) * R * C].bitcast(F32).rearrange("s (r c) -> s r c", r=R)
                  for j in range(SLOTS - 2)]
        w_hi = sb("w_hi", [P, CT, C], F32R)
        w_lo = sb("w_lo", [P, CT, C], F32R)
        bv = sb("bv", [P, CT])
        gamma = sb("gamma", [P, 1])
        gamma_bv = sb("gamma_bv", [P, CT])
        ident = sb("ident_b", [H, H])
        att = [x_res[j // 2][0:H, :, :].rearrange("p t n -> p (t n)")[:, j % 2 * C:(j % 2 + 1) * C]
               for j in range(4)]

        ps = ctx.enter_context(nc.psum_tensor("ps_b", [P, 8, BANK], F32))

        passed = ctx.enter_context(nc.semaphore("passed"))
        params_in = ctx.enter_context(nc.semaphore("params_in"))
        w_split = ctx.enter_context(nc.semaphore("w_split"))
        scaled_bias = ctx.enter_context(nc.semaphore("scaled_bias"))
        cols_in = [sem(f"cols_in{k}") for k in range(SLOTS)]
        rows_in = [sem(f"rows_in{p}") for p in range(2)]
        res_in = [sem(f"res_in{p}") for p in range(2)]
        cols_mm = [sem(f"cols_mm{k}") for k in range(SLOTS)]
        att_kept = [sem(f"att_kept{j}") for j in range(4)]
        att_turned = [sem(f"att_turned{j}") for j in range(4)]
        cols_act = sem("cols_act")
        cols_dve = sem("cols_dve")
        rows_mm = sem("rows_mm")
        summed = sem("summed")
        hi_done = [sem(f"hi_done{p}") for p in range(2)]
        lo_done = [sem(f"lo_done{p}") for p in range(2)]
        proj_mm = [sem(f"proj_mm{p}") for p in range(2)]
        affine_done = sem("affine_done")
        final_done = sem("final_done")
        stored = sem("stored")

        w_raw = y[:, 0, 0:CT * C].rearrange("p (t o) -> p t o", t=CT)

        def apart(eng):
            eng.sem_inc(passed, 1)

        def loop(eng, n, body):
            with eng.Fori(0, n) as i:
                body(i)

        def column(at, k, r):
            c = k * R + r
            return c % 4, at * (SLOTS * R // 4) + c // 4

        def pipelined(eng, b, ahead, behind):
            ahead(b * FOURS, 0)

            def body(i):
                for k in range(SLOTS):
                    ahead(b * FOURS + i + (k + 1) // SLOTS, (k + 1) % SLOTS)
                    behind(b * FOURS + i, i * SLOTS + k, k)
            loop(eng, FOURS - 1, body)
            for k in range(SLOTS):
                if k + 1 < SLOTS:
                    ahead((b + 1) * FOURS - 1, k + 1)
                behind((b + 1) * FOURS - 1, NU - SLOTS + k, k)

        def pixels(t0, t1, first):
            return y[:, t0:t1, bass.ds(first * W, UP)]

        block = ctx.enter_context(nc.Block())

        @block.sync
        def _(sp):
            sp.dma_start(w_raw, wv_t.rearrange("(t p) o -> p t o", p=P)).then_inc(params_in, 16)
            sp.dma_start(bv[:, :], bv_d).then_inc(params_in, 16)
            sp.dma_start(gamma[:, :], gamma_d).then_inc(params_in, 16)
            sp.dma_start(ident[:, :], ident_d[0:H, 0:H]).then_inc(params_in, 16)

            def load_cols(b, u, at, k):
                sp.wait_ge(cols_mm[k], FROM + at * R)
                sp.dma_start(xt_in[k], x_t[bass.ds(b, 1), :, bass.ds(u * R, R), :].rearrange(
                    "b h w c -> h (b w) c")).then_inc(cols_in[k], 16)
                sp.dma_start(probs[k][:, :, :], col_probs[bass.ds(b, 1), :, bass.ds(u * R, R), :].rearrange(
                    "b g w h -> g (b w) h")).then_inc(cols_in[k], 16)

            def load_rows(b, u, p):
                sp.dma_start(xt_in[p], x_t[bass.ds(b, 1), bass.ds(u * R, R), :, :].rearrange(
                    "b h w c -> w (b h) c")).then_inc(rows_in[p], 16)
                sp.dma_start(probs[p][:, :, :], row_probs[bass.ds(b, 1), :, bass.ds(u * R, R), :].rearrange(
                    "b v h w -> v (b h) w")).then_inc(rows_in[p], 16)

            def load_res(b, u, p):
                sp.dma_start(x_res[p][:, :, :], x[bass.ds(b, 1), :, bass.ds(u * R, R), :].rearrange(
                    "b (t p) h w -> p (b t) (h w)", p=P)).then_inc(res_in[p], 16)

            def store(b, u):
                sp.wait_ge(final_done, FROM + b * NU + u + 1)
                sp.dma_start(out[bass.ds(b, 1), :, bass.ds(u * R, R), :].rearrange(
                    "b (t p) h w -> p (b t) (h w)", p=P), pixels(0, CT, u * R)).then_inc(stored, 16)

            def image(b):
                sp.wait_ge(rows_mm, FROM + b * NU * 2)
                for k in range(2):
                    load_cols(b, k, b * FOURS, k)
                for p in range(2):
                    sp.wait_ge(proj_mm[p], FROM + b * PAIRS * CT)
                for k in range(2, SLOTS):
                    load_cols(b, k, b * FOURS, k)

                def cols(i):
                    for k in range(SLOTS):
                        load_cols(b, i * SLOTS + k + SLOTS, b * FOURS + i + 1, k)
                loop(sp, FOURS - 1, cols)
                for k in range(2):
                    sp.wait_ge(cols_mm[k], FROM + (b + 1) * FOURS * R)
                    load_rows(b, k, k)
                for j in range(4):
                    sp.wait_ge(att_turned[j], FROM + (b + 1) * (NU * R // 4))
                for p in range(2):
                    load_res(b, p, p)
                sp.wait_ge(rows_mm, FROM + b * NU * 2 + 2)
                load_rows(b, 2, 0)

                def rows(i):
                    for p in range(2):
                        u = i * 2 + p
                        sp.wait_ge(rows_mm, FROM + (b * NU + u + 2) * 2)
                        load_rows(b, u + 3, 1 - p)
                        store(b, u)
                        load_res(b, u + 2, p)
                loop(sp, PAIRS - 2, rows)
                sp.wait_ge(rows_mm, FROM + (b * NU + NU - 2) * 2)
                load_rows(b, NU - 1, 1)
                store(b, NU - 4)
                load_res(b, NU - 2, 0)
                store(b, NU - 3)
                load_res(b, NU - 1, 1)
                for p in range(2):
                    store(b, NU - 2 + p)
            loop(sp, B, image)
            sp.wait_ge(stored, FROM + B * NU * 16)

        @block.tensor
        def _(pe):
            def attend_cols(at, k):
                pe.wait_ge(cols_in[k], FROM + (at + 1) * 32)
                for r in range(R):
                    bank, used = column(at, k, r)
                    pe.wait_ge(att_kept[bank], FROM + used)
                    nc.tensor.matmul(ps[0:H, bank, 0:C], probs[k][:, r, :], xt_in[k][:, r, :],
                                     start=True, stop=True).then_inc(cols_mm[k], 1)

            def turn_cols(at, u, k):
                unit = at * SLOTS + k
                pe.wait_ge(cols_act, FROM + unit)
                pe.wait_ge(cols_dve, FROM + unit)
                for r in range(R):
                    j, used = column(at, k, r)
                    pe.wait_ge(att_kept[j], FROM + used + 1)
                    for t in range(CT):
                        mm = nc.tensor.transpose(ps[:, CT + t, r * H:(r + 1) * H],
                                                 att[j][:, t * P:(t + 1) * P], ident[:, :])
                    mm.then_inc(att_turned[j], 1)

            def attend_rows(b, u, at, p):
                pe.wait_ge(rows_in[p], FROM + (at + 1) * 32)
                pe.wait_ge(summed, FROM + (b * NU + u) * 2)
                for t in range(CT):
                    for r in range(R):
                        mm = nc.tensor.matmul(ps[:, t, r * W:(r + 1) * W],
                                              xt_in[p][:, r, t * P:(t + 1) * P], probs[p][:, r, :],
                                              start=True, stop=True)
                    if t % 2:
                        mm.then_inc(rows_mm, 1)

            def project(b, u, at, p):
                pe.wait_ge(hi_done[p], FROM + (at + 1) * 2)
                pe.wait_ge(lo_done[p], FROM + (at + 1) * 2)
                for m in range(CT):
                    pe.wait_ge(affine_done, FROM + (b * NU + u) * CT)
                    cols = slice(m * P, (m + 1) * P)
                    n = 0
                    for t in range(CT):
                        for w, v in ((w_hi, y_hi), (w_hi, y_lo), (w_lo, y_hi)):
                            mm = nc.tensor.matmul(ps[:, CT + m, 0:UP], w[:, t, cols], v[p][:, t, :],
                                                  start=(n == 0), stop=(n == 3 * CT - 1))
                            n += 1
                    mm.then_inc(proj_mm[p], 1)

            pe.wait_ge(params_in, 64)
            pe.wait_ge(w_split, 2)

            def image(b):
                at0 = b * PAIRS
                pe.wait_ge(affine_done, FROM + b * NU * CT)
                apart(pe)

                pipelined(pe, b, attend_cols, turn_cols)
                for j in range(4):
                    pe.wait_ge(att_kept[j], FROM + (b + 1) * (NU * R // 4))
                pe.wait_ge(cols_act, FROM + (b + 1) * NU)
                pe.wait_ge(cols_dve, FROM + (b + 1) * NU)
                attend_rows(b, 0, at0, 0)

                def rows(i):
                    attend_rows(b, i * 2 + 1, at0 + i, 1)
                    project(b, i * 2, at0 + i, 0)
                    attend_rows(b, i * 2 + 2, at0 + i + 1, 0)
                    project(b, i * 2 + 1, at0 + i, 1)
                loop(pe, PAIRS - 1, rows)
                attend_rows(b, NU - 1, at0 + PAIRS - 1, 1)
                project(b, NU - 2, at0 + PAIRS - 1, 0)
                project(b, NU - 1, at0 + PAIRS - 1, 1)
            loop(pe, B, image)

        @block.scalar
        def _(act):
            act.wait_ge(params_in, 64)
            nc.scalar.activation(w_hi[:, :, :], w_raw, ACT.Copy).then_inc(w_split, 1)
            act.wait_ge(scaled_bias, 1)

            def keep_att(at, k):
                for r in range(R):
                    j, used = column(at, k, r)
                    if j % 2 == 0:
                        act.wait_ge(cols_mm[k], FROM + at * R + r + 1)
                        act.wait_ge(att_turned[j], FROM + used)
                        nc.scalar.activation(att[j], ps[0:H, j, 0:C], ACT.Copy).then_inc(att_kept[j], 1)

            def keep_cols(at, u, k):
                j, used = column(at, k, R - 1)
                act.wait_ge(att_turned[j], FROM + used + 1)
                for t in range(0, CT, 2):
                    copy = nc.scalar.activation(
                        y[:, t, :].rearrange("p (h w) -> p h w", h=H)[:, :, bass.ds(u * R, R)],
                        ps[:, CT + t, 0:UP].rearrange("p (w h) -> p h w", w=R), ACT.Copy)
                copy.then_inc(cols_act, 1)

            def high(b, u, at, p):
                act.wait_ge(proj_mm[p], FROM + at * CT)
                for j in range(2):
                    act.wait_ge(summed, FROM + (b * NU + u) * 2 + j + 1)
                    nc.scalar.activation(y_hi[p][:, 2 * j:2 * j + 2, :], pixels(2 * j, 2 * j + 2, u * R),
                                         ACT.Copy).then_inc(hi_done[p], 1)

            def affine(b, u, at, p):
                act.wait_ge(lo_done[p], FROM + (at + 1) * 2)
                act.wait_ge(hi_done[p], FROM + (at + 1) * 2)
                for m in range(CT):
                    act.wait_ge(proj_mm[p], FROM + at * CT + m + 1)
                    apart(act)
                    nc.scalar.activation(pixels(m, m + 1, u * R).rearrange("p a n -> p (a n)"), ps[:, CT + m, 0:UP],
                                         ACT.Identity, bias=gamma_bv[:, m:m + 1],
                                         scale=gamma[:, 0:1]).then_inc(affine_done, 1)

            def image(b):
                at0 = b * PAIRS
                act.wait_ge(stored, FROM + b * NU * 16)
                apart(act)

                pipelined(act, b, keep_att, keep_cols)
                high(b, 0, at0, 0)

                def rows(i):
                    high(b, i * 2 + 1, at0 + i, 1)
                    affine(b, i * 2, at0 + i, 0)
                    high(b, i * 2 + 2, at0 + i + 1, 0)
                    affine(b, i * 2 + 1, at0 + i, 1)
                loop(act, PAIRS - 1, rows)
                high(b, NU - 1, at0 + PAIRS - 1, 1)
                affine(b, NU - 2, at0 + PAIRS - 1, 0)
                affine(b, NU - 1, at0 + PAIRS - 1, 1)
            loop(act, B, image)

        @block.vector
        def _(dve):
            dve.wait_ge(params_in, 64)
            nc.vector.tensor_scalar(gamma_bv[:, :], bv[:, :], gamma[:, 0:1], None,
                                    ALU.mult).then_inc(scaled_bias, 1)
            dve.wait_ge(w_split, 1)
            nc.vector.tensor_tensor(w_lo[:, :, :], w_raw, w_hi[:, :, :].bitcast(F32),
                                    ALU.subtract).then_inc(w_split, 1)
            dve.wait_ge(w_split, 2)

            def keep_att(at, k):
                for r in range(R):
                    j, used = column(at, k, r)
                    if j % 2:
                        dve.wait_ge(cols_mm[k], FROM + at * R + r + 1)
                        dve.wait_ge(att_turned[j], FROM + used)
                        nc.vector.tensor_copy(att[j], ps[0:H, j, 0:C]).then_inc(att_kept[j], 1)

            def keep_cols(at, u, k):
                j, used = column(at, k, R - 1)
                dve.wait_ge(att_turned[j], FROM + used + 1)
                for t in range(1, CT, 2):
                    copy = nc.vector.tensor_copy(
                        y[:, t, :].rearrange("p (h w) -> p h w", h=H)[:, :, bass.ds(u * R, R)],
                        ps[:, CT + t, 0:UP].rearrange("p (w h) -> p h w", w=R))
                copy.then_inc(cols_dve, 1)

            def add_rows(b, u, at, p):
                for j in range(2):
                    dve.wait_ge(rows_mm, FROM + (b * NU + u) * 2 + j + 1)
                    part = pixels(2 * j, 2 * j + 2, u * R)
                    nc.vector.tensor_tensor(part, ps[:, 2 * j:2 * j + 2, 0:UP], part,
                                            ALU.add).then_inc(summed, 1)
                dve.wait_ge(proj_mm[p], FROM + at * CT)
                for j in range(2):
                    dve.wait_ge(summed, FROM + (b * NU + u) * 2 + j + 1)
                    dve.wait_ge(hi_done[p], FROM + at * 2 + j + 1)
                    nc.vector.tensor_tensor(y_lo[p][:, 2 * j:2 * j + 2, :], pixels(2 * j, 2 * j + 2, u * R),
                                            y_hi[p][:, 2 * j:2 * j + 2, :].bitcast(F32),
                                            ALU.subtract).then_inc(lo_done[p], 1)

            def image(b):
                at0 = b * PAIRS
                dve.wait_ge(stored, FROM + b * NU * 16)
                apart(dve)

                pipelined(dve, b, keep_att, keep_cols)
                dve.wait_ge(cols_act, FROM + (b + 1) * NU)
                dve.wait_ge(cols_dve, FROM + (b + 1) * NU)
                apart(dve)

                def rows(i):
                    for p in range(2):
                        add_rows(b, i * 2 + p, at0 + i, p)
                loop(dve, PAIRS, rows)
            loop(dve, B, image)

        @block.gpsimd
        def _(pool):
            for s in counted:
                pool.sem_inc(s, FROM)

            def image(b):
                def rows(i):
                    for p in range(2):
                        u = i * 2 + p
                        pool.wait_ge(res_in[p], FROM + (b * PAIRS + i + 1) * 16)
                        pool.wait_ge(affine_done, FROM + (b * NU + u + 1) * CT)
                        part = pixels(0, CT, u * R)
                        nc.gpsimd.tensor_tensor(part, part, x_res[p][:, :, :], ALU.add).then_inc(final_done, 1)
                loop(pool, PAIRS, rows)
            loop(pool, B, image)


def kernel(x, L0_conv_Wq, L0_conv_bq, L0_conv_Wk, L0_conv_bk, L0_conv_Wv, L0_conv_bv, L0_conv_gamma):
    import concourse.bacc as bacc
    from concourse.bass_utils import run_bass_kernel_spmd

    x = np.ascontiguousarray(x)
    wq, wk, wv = np.asarray(L0_conv_Wq), np.asarray(L0_conv_Wk), np.asarray(L0_conv_Wv)
    side = x.shape[2]
    arrays = {
        "x": x,
        "wqk_t": np.ascontiguousarray(np.concatenate([wq, wk]).T),
        "bias_q": np.ascontiguousarray(np.tile(np.asarray(L0_conv_bq), 2).reshape(P, 1)),
        "bias_k": np.ascontiguousarray(np.tile(np.asarray(L0_conv_bk), 2).reshape(P, 1)),
        "wv_t": np.ascontiguousarray(wv.T),
        "bv": np.ascontiguousarray(np.asarray(L0_conv_bv).reshape(-1, P).T),
        "gamma": np.ascontiguousarray(np.tile(np.asarray(L0_conv_gamma), P).reshape(P, 1)),
        "ident": np.eye(P, dtype=np.float32),
        "diag": np.where(np.eye(side, dtype=bool), np.float32(MASKED), np.float32(0)).astype(np.float32),
    }
    nc = bacc.Bacc("TRN2", target_bir_lowering=False, num_devices=1)
    args = [nc.dram_tensor(f"{n}_dram", a.shape, F32, kind="ExternalInput").ap() for n, a in arrays.items()]
    out = nc.dram_tensor("out_dram", x.shape, F32, kind="ExternalOutput").ap()
    build_program(nc, *args, out)
    r = run_bass_kernel_spmd(nc, [{f"{n}_dram": a for n, a in arrays.items()}], core_ids=[0])
    return r.results[0]["out_dram"]
```

```python
from contextlib import ExitStack

import numpy as np
import concourse.bass as bass
from concourse import mybir

F32 = mybir.dt.float32
F32R = mybir.dt.float32r
ALU = mybir.AluOpType
ACT = mybir.ActivationFunctionType
AX_X = mybir.AxisListType.X

P = 128
MASKED = -3.0e38
FROM = 1
BANK = 512


def build_program(nc, x, wkq_t, bias_kq, wv_t, bv, gamma, ident, diag, out):
    B, C, H, W = x.shape
    x_t = nc.dram_tensor("x_t", (B, H, W, C), F32).ap()
    row_probs = nc.dram_tensor("row_probs", (B, W, H, W), F32).ap()
    col_probs = nc.dram_tensor("col_probs", (B, H, W, H), F32).ap()
    attention_weights(nc, x, wkq_t, bias_kq, ident, diag, x_t, row_probs, col_probs)
    attend_and_project(nc, x, wv_t, bv, gamma, ident, x_t, row_probs, col_probs, out)


def attention_weights(nc, x, wkq_t, bias_kq, ident_d, diag_d, x_t, row_probs, col_probs):
    B, C, H, W = x.shape
    KT = C // P
    IC = wkq_t.shape[1] // 2
    R = 4
    BP = R * W
    SLOTS = 4
    BODIES = H // (R * SLOTS)
    NB = H // R
    HALF = BODIES // 2
    CH = H // (HALF * SLOTS)
    NCH = H // CH
    PER = CH // R
    assert H == W and CH * NCH == H and HALF * 2 == BODIES

    with ExitStack() as ctx:
        def sb(name, shape, dt=F32):
            return ctx.enter_context(nc.sbuf_tensor(name, shape, dt))

        counted = []

        def sem(name):
            counted.append(ctx.enter_context(nc.semaphore(name)))
            return counted[-1]

        x_in = [sb(f"x_in{k}", [P, KT, BP]) for k in range(SLOTS)]
        xt_out = [sb(f"xt_out{k}", [W, R, C]) for k in range(SLOTS)]
        wkq = sb("wkq", [P, KT, 2 * IC])
        bkq = sb("bkq", [P, 1])
        ident = sb("ident", [P, P])
        diag = sb("diag", [H, H])
        kq_all = sb("kq_all", [2 * IC, H, W])
        k_all = kq_all[0:IC, :, :]
        q_all = kq_all[IC:2 * IC, :, :]
        q_rows = [sb(f"q_rows{p}", [IC, R, W]) for p in range(2)]
        q_cols = [sb(f"q_cols{p}", [IC, R, H]) for p in range(2)]
        e_row = sb("e_row", [W, H, W])
        e_col = sb("e_col", [H, W, H])
        max_row = sb("max_row", [W, H])
        max_col = sb("max_col", [H, W])
        sum_row = sb("sum_row", [W, H])
        sum_col = sb("sum_col", [H, W])
        p_row_in = sb("p_row_in", [W, CH, W])
        p_col_in = sb("p_col_in", [H, CH, H])
        p_row_out = [sb(f"p_row_out{p}", [W, CH, W]) for p in range(2)]
        p_col_out = [sb(f"p_col_out{p}", [H, CH, H]) for p in range(2)]

        ps = ctx.enter_context(nc.psum_tensor("ps_a", [P, 8, BANK], F32))

        passed = ctx.enter_context(nc.semaphore("passed"))
        consts_in = ctx.enter_context(nc.semaphore("consts_in"))
        x_loaded = [sem(f"x_loaded{k}") for k in range(SLOTS)]
        kq_done = [sem(f"kq_done{k}") for k in range(SLOTS)]
        kq_kept = [sem(f"kq_kept{p}") for p in range(2)]
        xt_turned = [sem(f"xt_turned{p}") for p in range(2)]
        xt_kept = [sem(f"xt_kept{p}") for p in range(2)]
        xt_stored = [sem(f"xt_stored{k}") for k in range(SLOTS)]
        q_rows_laid = [sem(f"q_rows_laid{p}") for p in range(2)]
        q_cols_laid = [sem(f"q_cols_laid{p}") for p in range(2)]
        e_row_mm = [sem(f"e_row_mm{p}") for p in range(2)]
        e_col_mm = [sem(f"e_col_mm{p}") for p in range(2)]
        e_row_kept = [sem(f"e_row_kept{p}") for p in range(2)]
        e_col_kept = [sem(f"e_col_kept{p}") for p in range(2)]
        max_done = sem("max_done")
        stat_turned = sem("stat_turned")
        joint_done = sem("joint_done")
        total_done = sem("total_done")
        inv_done = sem("inv_done")
        shifted = sem("shifted")
        exp_done = sem("exp_done")
        sum_done = sem("sum_done")
        scaled_row = sem("scaled_row")
        scaled_col = sem("scaled_col")
        p_row_turned = [sem(f"p_row_turned{p}") for p in range(PER)]
        p_col_turned = [sem(f"p_col_turned{p}") for p in range(PER)]
        p_row_kept = [sem(f"p_row_kept{p}") for p in range(PER)]
        p_col_kept = [sem(f"p_col_kept{p}") for p in range(PER)]
        p_row_stored = [sem(f"p_row_stored{p}") for p in range(2)]
        p_col_stored = [sem(f"p_col_stored{p}") for p in range(2)]

        KQ_BANK, XT_BANK, ROW_BANK, COL_BANK = 0, 2, 4, 6
        UP = NB // 2

        def apart(eng):
            eng.sem_inc(passed, 1)

        def loop(eng, n, body):
            with eng.Fori(0, n) as i:
                body(i)

        block = ctx.enter_context(nc.Block())

        @block.sync
        def _(sp):
            sp.dma_start(wkq[:, :, :], wkq_t.rearrange("(t p) o -> p t o", p=P)).then_inc(consts_in, 16)
            sp.dma_start(bkq[:, :], bias_kq).then_inc(consts_in, 16)
            sp.dma_start(ident[:, :], ident_d).then_inc(consts_in, 16)
            sp.dma_start(diag[:, :], diag_d).then_inc(consts_in, 16)

            def image(b):
                def body(i):
                    for k in range(SLOTS):
                        sp.wait_ge(kq_done[k], FROM + b * BODIES + i)
                        sp.dma_start(
                            x_in[k][:, :, :],
                            x[bass.ds(b, 1), :, bass.ds(i * (SLOTS * R) + k * R, R), :].rearrange(
                                "b (t p) h w -> p (b t) (h w)", p=P)).then_inc(x_loaded[k], 16)
                loop(sp, BODIES, body)
            loop(sp, B, image)

        @block.tensor
        def _(pe):
            pe.wait_ge(consts_in, 4 * 16)

            def x_block(b, i, k, between=None):
                n = b * NB + i * SLOTS + k
                bank = k % 2
                used = (b * BODIES + i) * (SLOTS // 2) + k // 2
                pe.wait_ge(x_loaded[k], FROM + (b * BODIES + i + 1) * 16)
                for half in range(2):
                    for p in range(2):
                        r = 2 * half + p
                        pe.wait_ge(xt_kept[p], FROM + n * (R // 2) + half)
                        for t in range(KT):
                            mm = nc.tensor.transpose(ps[0:W, XT_BANK + p, t * P:(t + 1) * P],
                                                     x_in[k][:, t, r * W:(r + 1) * W], ident[:, :])
                        mm.then_inc(xt_turned[p], 1)
                    if half == 0:
                        pe.wait_ge(kq_kept[bank], FROM + used)
                    for t in range(half * KT // 2, (half + 1) * KT // 2):
                        mm = nc.tensor.matmul(ps[:, KQ_BANK + bank, 0:BP], wkq[:, t, :], x_in[k][:, t, :],
                                              start=(t == 0), stop=(t == KT - 1))
                    if half == 0 and between:
                        between()
                mm.then_inc(kq_done[k], 1)

            def energies(b):
                for p in range(2):
                    pe.wait_ge(kq_kept[p], FROM + (b + 1) * (NB // 2))
                apart(pe)

                def body(i):
                    for p in range(2):
                        at = b * UP + i
                        pe.wait_ge(q_rows_laid[p], FROM + at + 1)
                        pe.wait_ge(e_row_kept[p], FROM + at)
                        for r in range(R):
                            mm = nc.tensor.matmul(ps[0:W, ROW_BANK + p, r * W:(r + 1) * W],
                                                  q_rows[p][:, r, :],
                                                  k_all[:, bass.ds(i * (2 * R) + p * R + r, 1), :].rearrange(
                                                      "c a w -> c (a w)"), start=True, stop=True)
                        mm.then_inc(e_row_mm[p], 1)
                        pe.wait_ge(q_cols_laid[p], FROM + at + 1)
                        pe.wait_ge(e_col_kept[p], FROM + at)
                        for r in range(R):
                            mm = nc.tensor.matmul(ps[0:H, COL_BANK + p, r * H:(r + 1) * H],
                                                  q_cols[p][:, r, :],
                                                  k_all[:, :, bass.ds(i * (2 * R) + p * R + r, 1)].rearrange(
                                                      "c h a -> c (h a)"), start=True, stop=True)
                        mm.then_inc(e_col_mm[p], 1)
                loop(pe, UP, body)

            def turn_stats(row, col):
                nc.tensor.transpose(ps[0:H, ROW_BANK, 0:W], row[:, :], ident[0:W, 0:W]).then_inc(stat_turned, 1)
                nc.tensor.transpose(ps[0:W, COL_BANK, 0:H], col[:, :], ident[0:H, 0:H]).then_inc(stat_turned, 1)

            def turn_maxima(b):
                pe.wait_ge(max_done, FROM + (b + 1) * NB * 2)
                turn_stats(max_row, max_col)

            def turn_sums(b):
                pe.wait_ge(sum_done, FROM + (b + 1) * NCH * 2)
                turn_stats(sum_row, sum_col)

            def turn_probs(b, chunk):
                at = b * NCH + chunk
                pe.wait_ge(scaled_row, FROM + at + 1)
                for p in range(PER):
                    pe.wait_ge(p_row_kept[p], FROM + at)
                    for r in range(R):
                        mm = nc.tensor.transpose(
                            ps[0:W, ROW_BANK + p, r * W:(r + 1) * W],
                            p_row_in[:, p * R + r, :], ident[0:W, 0:W])
                    mm.then_inc(p_row_turned[p], 1)
                pe.wait_ge(scaled_col, FROM + at + 1)
                for p in range(PER):
                    pe.wait_ge(p_col_kept[p], FROM + at)
                    for r in range(R):
                        mm = nc.tensor.transpose(
                            ps[0:H, COL_BANK + p, r * H:(r + 1) * H],
                            p_col_in[:, p * R + r, :], ident[0:H, 0:H])
                    mm.then_inc(p_col_turned[p], 1)

            def drained(b):
                for p in range(PER):
                    pe.wait_ge(p_row_kept[p], FROM + (b + 1) * NCH)
                    pe.wait_ge(p_col_kept[p], FROM + (b + 1) * NCH)

            def first(i):
                for k in range(SLOTS):
                    x_block(0, i, k)
            loop(pe, BODIES, first)
            energies(0)
            turn_maxima(0)

            def image(c):
                b = c + 1
                def exps(i):
                    for k in range(SLOTS):
                        x_block(b, i, k)
                loop(pe, HALF, exps)
                turn_sums(c)
                pe.wait_ge(total_done, FROM + b * 2)
                apart(pe)

                def norms(i):
                    for k in range(SLOTS):
                        x_block(b, i + HALF, k, lambda: turn_probs(c, i * SLOTS + k))
                loop(pe, HALF, norms)
                drained(c)
                energies(b)
                turn_maxima(b)
            if B > 1:
                loop(pe, B - 1, image)
            turn_sums(B - 1)
            pe.wait_ge(total_done, FROM + B * 2)

            def last(i):
                for k in range(SLOTS):
                    turn_probs(B - 1, i * SLOTS + k)
            loop(pe, HALF, last)

        @block.scalar
        def _(act):
            act.wait_ge(consts_in, 4 * 16)

            def x_block(b, i, k, softmax=None):
                n = b * NB + i * SLOTS + k
                bank = k % 2
                act.wait_ge(xt_stored[k], FROM + (b * BODIES + i) * 16)
                for r in range(0, R, 2):
                    act.wait_ge(xt_turned[0], FROM + n * (R // 2) + r // 2 + 1)
                    nc.scalar.activation(xt_out[k][:, r, :], ps[0:W, XT_BANK, 0:C],
                                         ACT.Copy).then_inc(xt_kept[0], 1)
                    if r == 0 and softmax:
                        softmax()
                act.wait_ge(kq_done[k], FROM + b * BODIES + i + 1)
                nc.scalar.activation(
                    kq_all[:, bass.ds(i * (SLOTS * R) + k * R, R), :].rearrange("c h w -> c (h w)"),
                    ps[:, KQ_BANK + bank, 0:BP], ACT.Identity,
                    bias=bkq[:, 0:1], scale=1.0).then_inc(kq_kept[bank], 1)
                act.wait_ge(xt_kept[0], FROM + (n + 1) * (R // 2))
                act.wait_ge(xt_kept[1], FROM + (n + 1) * (R // 2))
                act.dma_start(
                    x_t[bass.ds(b, 1), bass.ds(i * (SLOTS * R) + k * R, R), :, :].rearrange(
                        "b h w c -> w (b h) c"), xt_out[k][:, :, :]).then_inc(xt_stored[k], 16)

            def energies(b):
                def lay_rows(i, p):
                    act.wait_ge(e_row_mm[p], FROM + b * UP + i)
                    apart(act)
                    nc.scalar.activation(
                        q_rows[p][:, :, :].rearrange("c h w -> c (h w)"),
                        q_all[:, bass.ds(i * (2 * R) + p * R, R), :].rearrange("c h w -> c (h w)"),
                        ACT.Copy).then_inc(q_rows_laid[p], 1)

                def keep(i, p):
                    act.wait_ge(e_row_mm[p], FROM + b * UP + i + 1)
                    apart(act)
                    nc.scalar.activation(
                        e_row[:, bass.ds(i * (2 * R) + p * R, R), :].rearrange("w h v -> w (h v)"),
                        ps[0:W, ROW_BANK + p, 0:BP], ACT.Copy).then_inc(e_row_kept[p], 1)

                for p in range(2):
                    act.wait_ge(kq_kept[p], FROM + (b + 1) * (NB // 2))
                lay_rows(0, 0)

                def body(i):
                    lay_rows(i, 1)
                    keep(i, 0)
                    lay_rows(i + 1, 0)
                    keep(i, 1)
                loop(act, UP - 1, body)
                lay_rows(UP - 1, 1)
                keep(UP - 1, 0)
                keep(UP - 1, 1)

            def exps(b, chunk):
                at = b * NCH + chunk
                for j, e in enumerate((e_row, e_col)):
                    act.wait_ge(shifted, FROM + at * 2 + j + 1)
                    apart(act)
                    part = e[:, bass.ds(chunk * CH, CH), :].rearrange("a b c -> a (b c)")
                    nc.scalar.activation(part, part, ACT.Exp).then_inc(exp_done, 1)

            def chunk_out(b, i, k):
                return k % 2, b * (NCH // 2) + i * (SLOTS // 2) + k // 2

            def keep_rows(b, i, k):
                at = b * NCH + i * SLOTS + k
                tile, used = chunk_out(b, i, k)
                act.wait_ge(p_row_stored[tile], FROM + used * 16)
                for p in range(PER):
                    act.wait_ge(p_row_turned[p], FROM + at + 1)
                    nc.scalar.activation(
                        p_row_out[tile][:, p * R:(p + 1) * R, :].rearrange("v h w -> v (h w)"),
                        ps[0:W, ROW_BANK + p, 0:BP], ACT.Copy).then_inc(p_row_kept[p], 1)

            def store_probs(b, i, k):
                at = b * NCH + i * SLOTS + k
                tile, _ = chunk_out(b, i, k)
                for p in range(PER):
                    act.wait_ge(p_row_kept[p], FROM + at + 1)
                apart(act)
                act.dma_start(
                    row_probs[bass.ds(b, 1), :, bass.ds(i * (SLOTS * CH) + k * CH, CH), :].rearrange(
                        "b v h w -> v (b h) w"), p_row_out[tile][:, :, :]).then_inc(p_row_stored[tile], 16)
                for p in range(PER):
                    act.wait_ge(p_col_kept[p], FROM + at + 1)
                apart(act)
                act.dma_start(
                    col_probs[bass.ds(b, 1), :, bass.ds(i * (SLOTS * CH) + k * CH, CH), :].rearrange(
                        "b g w h -> g (b w) h"), p_col_out[tile][:, :, :]).then_inc(p_col_stored[tile], 16)

            def first(i):
                for k in range(SLOTS):
                    x_block(0, i, k)
            loop(act, BODIES, first)
            energies(0)

            def image(c):
                b = c + 1
                for p in range(2):
                    act.wait_ge(e_row_mm[p], FROM + b * UP)
                    act.wait_ge(e_col_mm[p], FROM + b * UP)
                apart(act)

                def exp_body(i):
                    for k in range(SLOTS):
                        x_block(b, i, k, lambda: exps(c, i * SLOTS + k))
                loop(act, HALF, exp_body)

                def norm_body(i):
                    for k in range(SLOTS):
                        x_block(b, i + HALF, k, lambda: keep_rows(c, i, k))
                        store_probs(c, i, k)
                loop(act, HALF, norm_body)
                energies(b)
            if B > 1:
                loop(act, B - 1, image)

            def last_exps(i):
                for k in range(SLOTS):
                    exps(B - 1, i * SLOTS + k)
            loop(act, HALF, last_exps)

            def last_probs(i):
                for k in range(SLOTS):
                    keep_rows(B - 1, i, k)
                    store_probs(B - 1, i, k)
            loop(act, HALF, last_probs)
            for p in range(2):
                act.wait_ge(p_row_stored[p], FROM + B * NCH // 2 * 16)
                act.wait_ge(p_col_stored[p], FROM + B * NCH // 2 * 16)
            for k in range(SLOTS):
                act.wait_ge(xt_stored[k], FROM + B * BODIES * 16)

        @block.vector
        def _(dve):
            dve.wait_ge(consts_in, 4 * 16)

            def x_block(b, i, k, softmax=lambda part: None):
                n = b * NB + i * SLOTS + k
                dve.wait_ge(xt_stored[k], FROM + (b * BODIES + i) * 16)
                for r in range(1, R, 2):
                    dve.wait_ge(xt_turned[1], FROM + n * (R // 2) + r // 2 + 1)
                    nc.vector.tensor_copy(xt_out[k][:, r, :],
                                          ps[0:W, XT_BANK + 1, 0:C]).then_inc(xt_kept[1], 1)
                    softmax(r // 2)

            def energies(b):
                def lay_cols(i, p):
                    dve.wait_ge(e_col_mm[p], FROM + b * UP + i)
                    nc.vector.tensor_copy(
                        q_cols[p][:, :, :],
                        q_all[:, :, bass.ds(i * (2 * R) + p * R, R)].rearrange("c h w -> c w h")
                    ).then_inc(q_cols_laid[p], 1)

                def keep(i, p):
                    at = b * UP + i
                    first = i * (2 * R) + p * R
                    dve.wait_ge(e_col_mm[p], FROM + at + 1)
                    part = e_col[:, bass.ds(first, R), :]
                    nc.vector.tensor_tensor(
                        part, ps[0:H, COL_BANK + p, 0:BP].rearrange("h (w g) -> h w g", w=R),
                        diag[:, :].unsqueeze(1).to_broadcast([H, R, H]), ALU.add).then_inc(e_col_kept[p], 1)
                    dve.wait_ge(e_row_kept[p], FROM + at + 1)
                    nc.vector.tensor_reduce(max_row[:, bass.ds(first, R)], e_row[:, bass.ds(first, R), :],
                                            AX_X, ALU.max).then_inc(max_done, 1)
                    dve.wait_ge(e_col_kept[p], FROM + at + 1)
                    nc.vector.tensor_reduce(max_col[:, bass.ds(first, R)], part,
                                            AX_X, ALU.max).then_inc(max_done, 1)

                for p in range(2):
                    dve.wait_ge(kq_kept[p], FROM + (b + 1) * (NB // 2))
                lay_cols(0, 0)

                def body(i):
                    lay_cols(i, 1)
                    keep(i, 0)
                    lay_cols(i + 1, 0)
                    keep(i, 1)
                loop(dve, UP - 1, body)
                lay_cols(UP - 1, 1)
                keep(UP - 1, 0)
                keep(UP - 1, 1)

            def join_maxima(b):
                dve.wait_ge(stat_turned, FROM + b * 4 + 2)
                nc.vector.tensor_tensor(max_col[:, :], ps[0:H, ROW_BANK, 0:W], max_col[:, :],
                                        ALU.max).then_inc(joint_done, 1)
                nc.vector.tensor_tensor(max_row[:, :], ps[0:W, COL_BANK, 0:H], max_row[:, :],
                                        ALU.max).then_inc(joint_done, 1)

            def join_sums(b):
                dve.wait_ge(stat_turned, FROM + b * 4 + 4)
                nc.vector.tensor_tensor(sum_col[:, :], ps[0:H, ROW_BANK, 0:W], sum_col[:, :],
                                        ALU.add).then_inc(total_done, 1)
                nc.vector.tensor_tensor(sum_row[:, :], ps[0:W, COL_BANK, 0:H], sum_row[:, :],
                                        ALU.add).then_inc(total_done, 1)
                dve.wait_ge(total_done, FROM + b * 2 + 2)
                nc.vector.reciprocal(sum_row[:, :], sum_row[:, :]).then_inc(inv_done, 1)
                nc.vector.reciprocal(sum_col[:, :], sum_col[:, :]).then_inc(inv_done, 1)
                dve.wait_ge(inv_done, FROM + b * 2 + 2)
                apart(dve)

            def sums(b, chunk, j):
                at = b * NCH + chunk
                e, total = ((e_row, sum_row), (e_col, sum_col))[j]
                dve.wait_ge(exp_done, FROM + at * 2 + j + 1)
                nc.vector.tensor_reduce(total[:, bass.ds(chunk * CH, CH)], e[:, bass.ds(chunk * CH, CH), :],
                                        AX_X, ALU.add).then_inc(sum_done, 1)

            def scale_cols(b, chunk):
                at = b * NCH + chunk
                for p in range(PER):
                    dve.wait_ge(p_col_turned[p], FROM + at)
                nc.vector.tensor_tensor(
                    p_col_in[:, :, :], e_col[:, bass.ds(chunk * CH, CH), :],
                    sum_col[:, bass.ds(chunk * CH, CH)].unsqueeze(2).to_broadcast([H, CH, H]),
                    ALU.mult).then_inc(scaled_col, 1)

            def keep_probs(b, i, k):
                at = b * NCH + i * SLOTS + k
                tile, used = k % 2, b * (NCH // 2) + i * (SLOTS // 2) + k // 2
                dve.wait_ge(p_col_stored[tile], FROM + used * 16)
                for p in range(PER):
                    dve.wait_ge(p_col_turned[p], FROM + at + 1)
                    nc.vector.tensor_copy(
                        p_col_out[tile][:, p * R:(p + 1) * R, :].rearrange("g w h -> g (w h)"),
                        ps[0:H, COL_BANK + p, 0:BP]).then_inc(p_col_kept[p], 1)

            def first(i):
                for k in range(SLOTS):
                    x_block(0, i, k)
            loop(dve, BODIES, first)
            energies(0)
            join_maxima(0)

            def image(c):
                b = c + 1

                def exp_body(i):
                    for k in range(SLOTS):
                        x_block(b, i, k, lambda j: sums(c, i * SLOTS + k, j))
                loop(dve, HALF, exp_body)
                join_sums(c)

                def norm_body(i):
                    for k in range(SLOTS):
                        scale_cols(c, i * SLOTS + k)
                        x_block(b, i + HALF, k, lambda j: keep_probs(c, i, k) if j == 0 else None)
                loop(dve, HALF, norm_body)
                energies(b)
                join_maxima(b)
            if B > 1:
                loop(dve, B - 1, image)

            def last_sums(i):
                for k in range(SLOTS):
                    for j in range(2):
                        sums(B - 1, i * SLOTS + k, j)
            loop(dve, HALF, last_sums)
            join_sums(B - 1)

            def last_probs(i):
                for k in range(SLOTS):
                    scale_cols(B - 1, i * SLOTS + k)
                    keep_probs(B - 1, i, k)
            loop(dve, HALF, last_probs)

        @block.gpsimd
        def _(pool):
            for s in counted:
                pool.sem_inc(s, FROM)

            def shift(b):
                pool.wait_ge(joint_done, FROM + (b + 1) * 2)
                apart(pool)

                def body(i):
                    for k in range(SLOTS):
                        chunk = i * SLOTS + k
                        for e, m in ((e_row, max_row), (e_col, max_col)):
                            part = e[:, bass.ds(chunk * CH, CH), :]
                            nc.gpsimd.tensor_tensor(
                                part, part, m[:, bass.ds(chunk * CH, CH)].unsqueeze(2).to_broadcast([H, CH, H]),
                                ALU.subtract).then_inc(shifted, 1)
                loop(pool, HALF, body)

            def scale_rows(b):
                pool.wait_ge(inv_done, FROM + (b + 1) * 2)
                apart(pool)

                def body(i):
                    for k in range(SLOTS):
                        chunk = i * SLOTS + k
                        for p in range(PER):
                            pool.wait_ge(p_row_turned[p], FROM + b * NCH + chunk)
                        nc.gpsimd.tensor_tensor(
                            p_row_in[:, :, :], e_row[:, bass.ds(chunk * CH, CH), :],
                            sum_row[:, bass.ds(chunk * CH, CH)].unsqueeze(2).to_broadcast([W, CH, W]),
                            ALU.mult).then_inc(scaled_row, 1)
                loop(pool, HALF, body)

            def image(b):
                shift(b)
                scale_rows(b)
            loop(pool, B, image)


def attend_and_project(nc, x, wv_t, bv_d, gamma_d, ident_d, x_t, row_probs, col_probs, out):
    B, C, H, W = x.shape
    CT = C // P
    R = 3
    UP = R * W
    NU = H // R
    PAIRS = NU // 2
    SLOTS = 4
    FOURS = NU // SLOTS
    assert H == W and NU % SLOTS == 0 and (SLOTS - 2) * R * C <= 4 * CT * UP

    with ExitStack() as ctx:
        def sb(name, shape, dt=F32):
            return ctx.enter_context(nc.sbuf_tensor(name, shape, dt))

        counted = []

        def sem(name):
            counted.append(ctx.enter_context(nc.semaphore(name)))
            return counted[-1]

        y = sb("y", [P, CT, H * W])
        probs = [sb(f"probs{p}", [H, R, W]) for p in range(SLOTS)]
        x_res = [sb(f"x_res{p}", [P, CT, UP]) for p in range(2)]
        parts = sb("parts", [P, 4 * CT * UP], F32R)

        def part(j):
            return parts[:, j * CT * UP:(j + 1) * CT * UP].rearrange("p (t n) -> p t n", t=CT)
        y_hi = [part(0), part(1)]
        y_lo = [part(2), part(3)]
        xt_in = [sb(f"xt_in{p}", [H, R, C])[:, :, :] for p in range(2)]
        xt_in += [parts[0:H, j * R * C:(j + 1) * R * C].bitcast(F32).rearrange("s (r c) -> s r c", r=R)
                  for j in range(SLOTS - 2)]
        w_hi = sb("w_hi", [P, CT, C], F32R)
        w_lo = sb("w_lo", [P, CT, C], F32R)
        bv = sb("bv", [P, CT])
        gamma = sb("gamma", [P, 1])
        gamma_bv = sb("gamma_bv", [P, CT])
        ident = sb("ident_b", [H, H])
        att = [x_res[j // 2][0:H, :, :].rearrange("p t n -> p (t n)")[:, j % 2 * C:(j % 2 + 1) * C]
               for j in range(4)]

        ps = ctx.enter_context(nc.psum_tensor("ps_b", [P, 8, BANK], F32))

        passed = ctx.enter_context(nc.semaphore("passed"))
        params_in = ctx.enter_context(nc.semaphore("params_in"))
        w_split = ctx.enter_context(nc.semaphore("w_split"))
        scaled_bias = ctx.enter_context(nc.semaphore("scaled_bias"))
        cols_in = [sem(f"cols_in{k}") for k in range(SLOTS)]
        rows_in = [sem(f"rows_in{p}") for p in range(2)]
        res_in = [sem(f"res_in{p}") for p in range(2)]
        cols_mm = [sem(f"cols_mm{k}") for k in range(SLOTS)]
        att_kept = [sem(f"att_kept{j}") for j in range(4)]
        att_turned = [sem(f"att_turned{j}") for j in range(4)]
        cols_act = sem("cols_act")
        cols_dve = sem("cols_dve")
        rows_mm = sem("rows_mm")
        summed = sem("summed")
        hi_done = [sem(f"hi_done{p}") for p in range(2)]
        lo_done = [sem(f"lo_done{p}") for p in range(2)]
        proj_mm = [sem(f"proj_mm{p}") for p in range(2)]
        affine_done = sem("affine_done")
        final_done = sem("final_done")
        stored = sem("stored")

        w_raw = y[:, 0, 0:CT * C].rearrange("p (t o) -> p t o", t=CT)

        def apart(eng):
            eng.sem_inc(passed, 1)

        def loop(eng, n, body):
            with eng.Fori(0, n) as i:
                body(i)

        def column(at, k, r):
            c = k * R + r
            return c % 4, at * (SLOTS * R // 4) + c // 4

        def pipelined(eng, b, ahead, behind, free):
            ahead(b * FOURS, 0)
            free()
            apart(eng)

            def body(i):
                for k in range(SLOTS):
                    ahead(b * FOURS + i + (k + 1) // SLOTS, (k + 1) % SLOTS)
                    behind(b * FOURS + i, i * SLOTS + k, k)
            loop(eng, FOURS - 1, body)
            for k in range(SLOTS):
                if k + 1 < SLOTS:
                    ahead((b + 1) * FOURS - 1, k + 1)
                behind((b + 1) * FOURS - 1, NU - SLOTS + k, k)

        def pixels(t0, t1, first):
            return y[:, t0:t1, bass.ds(first * W, UP)]

        block = ctx.enter_context(nc.Block())

        @block.sync
        def _(sp):
            sp.dma_start(w_raw, wv_t.rearrange("(t p) o -> p t o", p=P)).then_inc(params_in, 16)
            sp.dma_start(bv[:, :], bv_d).then_inc(params_in, 16)
            sp.dma_start(gamma[:, :], gamma_d).then_inc(params_in, 16)
            sp.dma_start(ident[:, :], ident_d[0:H, 0:H]).then_inc(params_in, 16)

            def load_cols(b, u, at, k):
                sp.wait_ge(cols_mm[k], FROM + at * R)
                sp.dma_start(xt_in[k], x_t[bass.ds(b, 1), :, bass.ds(u * R, R), :].rearrange(
                    "b h w c -> h (b w) c")).then_inc(cols_in[k], 16)
                sp.dma_start(probs[k][:, :, :], col_probs[bass.ds(b, 1), :, bass.ds(u * R, R), :].rearrange(
                    "b g w h -> g (b w) h")).then_inc(cols_in[k], 16)

            def load_rows(b, u, p):
                sp.dma_start(xt_in[p], x_t[bass.ds(b, 1), bass.ds(u * R, R), :, :].rearrange(
                    "b h w c -> w (b h) c")).then_inc(rows_in[p], 16)
                sp.dma_start(probs[p][:, :, :], row_probs[bass.ds(b, 1), :, bass.ds(u * R, R), :].rearrange(
                    "b v h w -> v (b h) w")).then_inc(rows_in[p], 16)

            def load_res(b, u, p):
                sp.dma_start(x_res[p][:, :, :], x[bass.ds(b, 1), :, bass.ds(u * R, R), :].rearrange(
                    "b (t p) h w -> p (b t) (h w)", p=P)).then_inc(res_in[p], 16)

            def store(b, u):
                sp.wait_ge(final_done, FROM + b * NU + u + 1)
                sp.dma_start(out[bass.ds(b, 1), :, bass.ds(u * R, R), :].rearrange(
                    "b (t p) h w -> p (b t) (h w)", p=P), pixels(0, CT, u * R)).then_inc(stored, 16)

            def image(b, more):
                def cols(i):
                    for k in range(SLOTS):
                        load_cols(b, i * SLOTS + k + SLOTS, b * FOURS + i + 1, k)
                loop(sp, FOURS - 1, cols)
                for k in range(2):
                    sp.wait_ge(cols_mm[k], FROM + (b + 1) * FOURS * R)
                    load_rows(b, k, k)
                for j in range(4):
                    sp.wait_ge(att_turned[j], FROM + (b + 1) * (NU * R // 4))
                for p in range(2):
                    load_res(b, p, p)
                sp.wait_ge(rows_mm, FROM + b * NU * 2 + 2)
                load_rows(b, 2, 0)

                def rows(i):
                    for p in range(2):
                        u = i * 2 + p
                        sp.wait_ge(rows_mm, FROM + (b * NU + u + 2) * 2)
                        load_rows(b, u + 3, 1 - p)
                        store(b, u)
                        load_res(b, u + 2, p)
                loop(sp, PAIRS - 2, rows)
                sp.wait_ge(rows_mm, FROM + (b * NU + NU - 2) * 2)
                load_rows(b, NU - 1, 1)
                store(b, NU - 4)
                load_res(b, NU - 2, 0)
                store(b, NU - 3)
                load_res(b, NU - 1, 1)
                if more:
                    for k in range(2):
                        sp.wait_ge(rows_mm, FROM + (b * NU + NU - 1 + k) * 2)
                        load_cols(b + 1, k, (b + 1) * FOURS, k)
                for p in range(2):
                    store(b, NU - 2 + p)
                if more:
                    for p in range(2):
                        sp.wait_ge(proj_mm[p], FROM + (b + 1) * PAIRS * CT)
                    for k in range(2, SLOTS):
                        load_cols(b + 1, k, (b + 1) * FOURS, k)
            for k in range(SLOTS):
                load_cols(0, k, 0, k)
            if B > 1:
                loop(sp, B - 1, lambda b: image(b, True))
            image(B - 1, False)
            sp.wait_ge(stored, FROM + B * NU * 16)

        @block.tensor
        def _(pe):
            def attend_cols(at, k):
                pe.wait_ge(cols_in[k], FROM + (at + 1) * 32)
                for r in range(R):
                    bank, used = column(at, k, r)
                    pe.wait_ge(att_kept[bank], FROM + used)
                    nc.tensor.matmul(ps[0:H, bank, 0:C], probs[k][:, r, :], xt_in[k][:, r, :],
                                     start=True, stop=True).then_inc(cols_mm[k], 1)

            def turn_cols(at, u, k):
                unit = at * SLOTS + k
                pe.wait_ge(cols_act, FROM + unit)
                pe.wait_ge(cols_dve, FROM + unit)
                for r in range(R):
                    j, used = column(at, k, r)
                    pe.wait_ge(att_kept[j], FROM + used + 1)
                    for t in range(CT):
                        mm = nc.tensor.transpose(ps[:, CT + t, r * H:(r + 1) * H],
                                                 att[j][:, t * P:(t + 1) * P], ident[:, :])
                    mm.then_inc(att_turned[j], 1)

            def attend_rows(b, u, at, p):
                pe.wait_ge(rows_in[p], FROM + (at + 1) * 32)
                pe.wait_ge(summed, FROM + (b * NU + u) * 2)
                for t in range(CT):
                    for r in range(R):
                        mm = nc.tensor.matmul(ps[:, t, r * W:(r + 1) * W],
                                              xt_in[p][:, r, t * P:(t + 1) * P], probs[p][:, r, :],
                                              start=True, stop=True)
                    if t % 2:
                        mm.then_inc(rows_mm, 1)

            def project(b, u, at, p):
                pe.wait_ge(hi_done[p], FROM + (at + 1) * 2)
                pe.wait_ge(lo_done[p], FROM + (at + 1) * 2)
                for m in range(CT):
                    pe.wait_ge(affine_done, FROM + (b * NU + u) * CT)
                    cols = slice(m * P, (m + 1) * P)
                    n = 0
                    for t in range(CT):
                        for w, v in ((w_hi, y_hi), (w_hi, y_lo), (w_lo, y_hi)):
                            mm = nc.tensor.matmul(ps[:, CT + m, 0:UP], w[:, t, cols], v[p][:, t, :],
                                                  start=(n == 0), stop=(n == 3 * CT - 1))
                            n += 1
                    mm.then_inc(proj_mm[p], 1)

            pe.wait_ge(params_in, 64)
            pe.wait_ge(w_split, 2)

            def image(b):
                at0 = b * PAIRS
                pe.wait_ge(summed, FROM + b * NU * 2)
                pipelined(pe, b, attend_cols, turn_cols,
                          lambda: pe.wait_ge(affine_done, FROM + b * NU * CT))
                for j in range(4):
                    pe.wait_ge(att_kept[j], FROM + (b + 1) * (NU * R // 4))
                pe.wait_ge(cols_act, FROM + (b + 1) * NU)
                pe.wait_ge(cols_dve, FROM + (b + 1) * NU)
                attend_rows(b, 0, at0, 0)

                def rows(i):
                    attend_rows(b, i * 2 + 1, at0 + i, 1)
                    project(b, i * 2, at0 + i, 0)
                    attend_rows(b, i * 2 + 2, at0 + i + 1, 0)
                    project(b, i * 2 + 1, at0 + i, 1)
                loop(pe, PAIRS - 1, rows)
                attend_rows(b, NU - 1, at0 + PAIRS - 1, 1)
                project(b, NU - 2, at0 + PAIRS - 1, 0)
                project(b, NU - 1, at0 + PAIRS - 1, 1)
            loop(pe, B, image)

        @block.scalar
        def _(act):
            act.wait_ge(params_in, 64)
            nc.scalar.activation(w_hi[:, :, :], w_raw, ACT.Copy).then_inc(w_split, 1)
            act.wait_ge(scaled_bias, 1)

            def keep_att(at, k):
                for r in range(R):
                    j, used = column(at, k, r)
                    if j % 2 == 0:
                        act.wait_ge(cols_mm[k], FROM + at * R + r + 1)
                        act.wait_ge(att_turned[j], FROM + used)
                        nc.scalar.activation(att[j], ps[0:H, j, 0:C], ACT.Copy).then_inc(att_kept[j], 1)

            def keep_cols(at, u, k):
                j, used = column(at, k, R - 1)
                act.wait_ge(att_turned[j], FROM + used + 1)
                for t in range(0, CT, 2):
                    copy = nc.scalar.activation(
                        y[:, t, :].rearrange("p (h w) -> p h w", h=H)[:, :, bass.ds(u * R, R)],
                        ps[:, CT + t, 0:UP].rearrange("p (w h) -> p h w", w=R), ACT.Copy)
                copy.then_inc(cols_act, 1)

            def high(b, u, at, p):
                act.wait_ge(proj_mm[p], FROM + at * CT)
                for j in range(2):
                    act.wait_ge(summed, FROM + (b * NU + u) * 2 + j + 1)
                    nc.scalar.activation(y_hi[p][:, 2 * j:2 * j + 2, :], pixels(2 * j, 2 * j + 2, u * R),
                                         ACT.Copy).then_inc(hi_done[p], 1)

            def affine(b, u, at, p):
                act.wait_ge(lo_done[p], FROM + (at + 1) * 2)
                act.wait_ge(hi_done[p], FROM + (at + 1) * 2)
                for m in range(CT):
                    act.wait_ge(proj_mm[p], FROM + at * CT + m + 1)
                    apart(act)
                    nc.scalar.activation(pixels(m, m + 1, u * R).rearrange("p a n -> p (a n)"), ps[:, CT + m, 0:UP],
                                         ACT.Identity, bias=gamma_bv[:, m:m + 1],
                                         scale=gamma[:, 0:1]).then_inc(affine_done, 1)

            def image(b):
                at0 = b * PAIRS
                act.wait_ge(final_done, FROM + b * NU)
                pipelined(act, b, keep_att, keep_cols,
                          lambda: act.wait_ge(stored, FROM + b * NU * 16))
                high(b, 0, at0, 0)

                def rows(i):
                    high(b, i * 2 + 1, at0 + i, 1)
                    affine(b, i * 2, at0 + i, 0)
                    high(b, i * 2 + 2, at0 + i + 1, 0)
                    affine(b, i * 2 + 1, at0 + i, 1)
                loop(act, PAIRS - 1, rows)
                high(b, NU - 1, at0 + PAIRS - 1, 1)
                affine(b, NU - 2, at0 + PAIRS - 1, 0)
                affine(b, NU - 1, at0 + PAIRS - 1, 1)
            loop(act, B, image)

        @block.vector
        def _(dve):
            dve.wait_ge(params_in, 64)
            nc.vector.tensor_scalar(gamma_bv[:, :], bv[:, :], gamma[:, 0:1], None,
                                    ALU.mult).then_inc(scaled_bias, 1)
            dve.wait_ge(w_split, 1)
            nc.vector.tensor_tensor(w_lo[:, :, :], w_raw, w_hi[:, :, :].bitcast(F32),
                                    ALU.subtract).then_inc(w_split, 1)
            dve.wait_ge(w_split, 2)

            def keep_att(at, k):
                for r in range(R):
                    j, used = column(at, k, r)
                    if j % 2:
                        dve.wait_ge(cols_mm[k], FROM + at * R + r + 1)
                        dve.wait_ge(att_turned[j], FROM + used)
                        nc.vector.tensor_copy(att[j], ps[0:H, j, 0:C]).then_inc(att_kept[j], 1)

            def keep_cols(at, u, k):
                j, used = column(at, k, R - 1)
                dve.wait_ge(att_turned[j], FROM + used + 1)
                for t in range(1, CT, 2):
                    copy = nc.vector.tensor_copy(
                        y[:, t, :].rearrange("p (h w) -> p h w", h=H)[:, :, bass.ds(u * R, R)],
                        ps[:, CT + t, 0:UP].rearrange("p (w h) -> p h w", w=R))
                copy.then_inc(cols_dve, 1)

            def add_rows(b, u, at, p):
                for j in range(2):
                    dve.wait_ge(rows_mm, FROM + (b * NU + u) * 2 + j + 1)
                    part = pixels(2 * j, 2 * j + 2, u * R)
                    nc.vector.tensor_tensor(part, ps[:, 2 * j:2 * j + 2, 0:UP], part,
                                            ALU.add).then_inc(summed, 1)
                dve.wait_ge(proj_mm[p], FROM + at * CT)
                for j in range(2):
                    dve.wait_ge(summed, FROM + (b * NU + u) * 2 + j + 1)
                    dve.wait_ge(hi_done[p], FROM + at * 2 + j + 1)
                    nc.vector.tensor_tensor(y_lo[p][:, 2 * j:2 * j + 2, :], pixels(2 * j, 2 * j + 2, u * R),
                                            y_hi[p][:, 2 * j:2 * j + 2, :].bitcast(F32),
                                            ALU.subtract).then_inc(lo_done[p], 1)

            def image(b):
                at0 = b * PAIRS
                dve.wait_ge(final_done, FROM + b * NU)
                pipelined(dve, b, keep_att, keep_cols,
                          lambda: dve.wait_ge(stored, FROM + b * NU * 16))
                dve.wait_ge(cols_act, FROM + (b + 1) * NU)
                dve.wait_ge(cols_dve, FROM + (b + 1) * NU)
                apart(dve)

                def rows(i):
                    for p in range(2):
                        add_rows(b, i * 2 + p, at0 + i, p)
                loop(dve, PAIRS, rows)
            loop(dve, B, image)

        @block.gpsimd
        def _(pool):
            for s in counted:
                pool.sem_inc(s, FROM)

            def image(b):
                def rows(i):
                    for p in range(2):
                        u = i * 2 + p
                        pool.wait_ge(res_in[p], FROM + (b * PAIRS + i + 1) * 16)
                        pool.wait_ge(affine_done, FROM + (b * NU + u + 1) * CT)
                        part = pixels(0, CT, u * R)
                        nc.gpsimd.tensor_tensor(part, part, x_res[p][:, :, :], ALU.add).then_inc(final_done, 1)
                loop(pool, PAIRS, rows)
            loop(pool, B, image)


def kernel(x, L0_conv_Wq, L0_conv_bq, L0_conv_Wk, L0_conv_bk, L0_conv_Wv, L0_conv_bv, L0_conv_gamma):
    import concourse.bacc as bacc
    from concourse.bass_utils import run_bass_kernel_spmd

    x = np.ascontiguousarray(x)
    wq, wk, wv = np.asarray(L0_conv_Wq), np.asarray(L0_conv_Wk), np.asarray(L0_conv_Wv)
    side = x.shape[2]
    arrays = {
        "x": x,
        "wkq_t": np.ascontiguousarray(np.concatenate([wk, wq]).T),
        "bias_kq": np.concatenate([np.asarray(L0_conv_bk), np.asarray(L0_conv_bq)]).reshape(P, 1),
        "wv_t": np.ascontiguousarray(wv.T),
        "bv": np.ascontiguousarray(np.asarray(L0_conv_bv).reshape(-1, P).T),
        "gamma": np.ascontiguousarray(np.tile(np.asarray(L0_conv_gamma), P).reshape(P, 1)),
        "ident": np.eye(P, dtype=np.float32),
        "diag": np.where(np.eye(side, dtype=bool), np.float32(MASKED), np.float32(0)).astype(np.float32),
    }
    nc = bacc.Bacc("TRN2", target_bir_lowering=False, num_devices=1)
    args = [nc.dram_tensor(f"{n}_dram", a.shape, F32, kind="ExternalInput").ap() for n, a in arrays.items()]
    out = nc.dram_tensor("out_dram", x.shape, F32, kind="ExternalOutput").ap()
    build_program(nc, *args, out)
    r = run_bass_kernel_spmd(nc, [{f"{n}_dram": a for n, a in arrays.items()}], core_ids=[0])
    return r.results[0]["out_dram"]
```

```python
from contextlib import ExitStack

import numpy as np
import concourse.bass as bass
from concourse import mybir

F32 = mybir.dt.float32
F32R = mybir.dt.float32r
ALU = mybir.AluOpType
ACT = mybir.ActivationFunctionType
AX_X = mybir.AxisListType.X

P = 128
MASKED = -3.0e38
FROM = 1
BANK = 512


def build_program(nc, x, wkq_t, bias_kq, wv_t, bv, gamma, ident, diag, out):
    B, C, H, W = x.shape
    x_t = nc.dram_tensor("x_t", (B, H, W, C), F32).ap()
    row_probs = nc.dram_tensor("row_probs", (B, W, H, W), F32).ap()
    col_probs = nc.dram_tensor("col_probs", (B, H, W, H), F32).ap()
    attention_weights(nc, x, wkq_t, bias_kq, ident, diag, x_t, row_probs, col_probs)
    attend_and_project(nc, x, wv_t, bv, gamma, ident, x_t, row_probs, col_probs, out)


def attention_weights(nc, x, wkq_t, bias_kq, ident_d, diag_d, x_t, row_probs, col_probs):
    B, C, H, W = x.shape
    KT = C // P
    IC = wkq_t.shape[1] // 2
    R = 4
    BP = R * W
    G = BP // P
    SLOTS = 4
    BODIES = H // (R * SLOTS)
    NB = H // R
    HALF = BODIES // 2
    CH = H // (HALF * SLOTS)
    NCH = H // CH
    PER = CH // R
    assert H == W and CH * NCH == H and HALF * 2 == BODIES and BP == G * P and SLOTS * G % 2 == 0

    with ExitStack() as ctx:
        def sb(name, shape, dt=F32):
            return ctx.enter_context(nc.sbuf_tensor(name, shape, dt))

        counted = []

        def sem(name):
            counted.append(ctx.enter_context(nc.semaphore(name)))
            return counted[-1]

        x_in = [sb(f"x_in{k}", [P, KT, BP]) for k in range(SLOTS)]
        xt_out = [sb(f"xt_out{k}", [P, G, C]) for k in range(SLOTS)]
        wkq = sb("wkq", [P, KT, 2 * IC])
        bkq = sb("bkq", [P, 1])
        ident = sb("ident", [P, P])
        diag = sb("diag", [H, H])
        kq_all = sb("kq_all", [2 * IC, H, W])
        k_all = kq_all[0:IC, :, :]
        q_all = kq_all[IC:2 * IC, :, :]
        q_rows = [sb(f"q_rows{p}", [IC, R, W]) for p in range(2)]
        q_cols = [sb(f"q_cols{p}", [IC, R, H]) for p in range(2)]
        e_row = sb("e_row", [W, H, W])
        e_col = sb("e_col", [H, W, H])
        max_row = sb("max_row", [W, H])
        max_col = sb("max_col", [H, W])
        sum_row = sb("sum_row", [W, H])
        sum_col = sb("sum_col", [H, W])
        p_row_in = [sb(f"p_row_in{p}", [W, CH, W]) for p in range(2)]
        p_col_in = [sb(f"p_col_in{p}", [H, CH, H]) for p in range(2)]
        p_row_out = [sb(f"p_row_out{k}", [W, CH, W]) for k in range(SLOTS)]
        p_col_out = [sb(f"p_col_out{k}", [H, CH, H]) for k in range(SLOTS)]

        ps = ctx.enter_context(nc.psum_tensor("ps_a", [P, 8, BANK], F32))

        passed = ctx.enter_context(nc.semaphore("passed"))
        consts_in = ctx.enter_context(nc.semaphore("consts_in"))
        x_loaded = [sem(f"x_loaded{k}") for k in range(SLOTS)]
        kq_done = [sem(f"kq_done{k}") for k in range(SLOTS)]
        kq_kept = [sem(f"kq_kept{p}") for p in range(2)]
        xt_turned = [sem(f"xt_turned{p}") for p in range(2)]
        xt_kept = [sem(f"xt_kept{p}") for p in range(2)]
        xt_stored = [sem(f"xt_stored{k}") for k in range(SLOTS)]
        q_rows_laid = [sem(f"q_rows_laid{p}") for p in range(2)]
        q_cols_laid = [sem(f"q_cols_laid{p}") for p in range(2)]
        e_row_mm = [sem(f"e_row_mm{p}") for p in range(2)]
        e_col_mm = [sem(f"e_col_mm{p}") for p in range(2)]
        e_row_kept = [sem(f"e_row_kept{p}") for p in range(2)]
        e_col_kept = [sem(f"e_col_kept{p}") for p in range(2)]
        max_done = sem("max_done")
        stat_turned = sem("stat_turned")
        joint_done = sem("joint_done")
        total_done = sem("total_done")
        inv_done = sem("inv_done")
        shifted = sem("shifted")
        exp_done = sem("exp_done")
        sum_done = sem("sum_done")
        scaled_row = sem("scaled_row")
        scaled_col = sem("scaled_col")
        p_row_turned = [[sem(f"p_row_turned{j}_{p}") for p in range(PER)] for j in range(2)]
        p_col_turned = [[sem(f"p_col_turned{j}_{p}") for p in range(PER)] for j in range(2)]
        p_row_kept = [sem(f"p_row_kept{p}") for p in range(PER)]
        p_col_kept = [sem(f"p_col_kept{p}") for p in range(PER)]
        p_row_stored = [sem(f"p_row_stored{k}") for k in range(SLOTS)]
        p_col_stored = [sem(f"p_col_stored{k}") for k in range(SLOTS)]

        KQ_BANK, XT_BANK, ROW_BANK, COL_BANK = 0, 2, 4, 6
        UP = NB // 2

        def turned(b, i, k, g):
            m = k * G + g
            return m % 2, (b * BODIES + i) * (SLOTS * G // 2) + m // 2

        def tile_of(b, i, k):
            return k % 2, b * (NCH // 2) + i * (SLOTS // 2) + k // 2

        def apart(eng):
            eng.sem_inc(passed, 1)

        def loop(eng, n, body):
            with eng.Fori(0, n) as i:
                body(i)

        block = ctx.enter_context(nc.Block())

        @block.sync
        def _(sp):
            sp.dma_start(wkq[:, :, :], wkq_t.rearrange("(t p) o -> p t o", p=P)).then_inc(consts_in, 16)
            sp.dma_start(bkq[:, :], bias_kq).then_inc(consts_in, 16)
            sp.dma_start(ident[:, :], ident_d).then_inc(consts_in, 16)
            sp.dma_start(diag[:, :], diag_d).then_inc(consts_in, 16)

            def load(b, i, k):
                sp.wait_ge(kq_done[k], FROM + b * BODIES + i)
                sp.dma_start(
                    x_in[k][:, :, :],
                    x[bass.ds(b, 1), :, bass.ds(i * (SLOTS * R) + k * R, R), :].rearrange(
                        "b (t p) h w -> p (b t) (h w)", p=P)).then_inc(x_loaded[k], 16)

            def store_turned(b, i, k):
                for g in range(G - 2, G):
                    bank, used = turned(b, i, k, g)
                    sp.wait_ge(xt_kept[bank], FROM + used + 1)
                    apart(sp)
                sp.dma_start(
                    x_t.rearrange("b h w c -> b (h w) c")[
                        bass.ds(b, 1), bass.ds(i * (SLOTS * BP) + k * BP, BP), :].rearrange(
                        "b (g p) c -> p (b g) c", p=P), xt_out[k][:, :, :]).then_inc(xt_stored[k], 16)

            def store_probs(b, i, k):
                at = b * NCH + i * SLOTS + k
                for p in range(PER):
                    sp.wait_ge(p_row_kept[p], FROM + at + 1)
                sp.dma_start(
                    row_probs[bass.ds(b, 1), :, bass.ds(i * (SLOTS * CH) + k * CH, CH), :].rearrange(
                        "b v h w -> v (b h) w"), p_row_out[k][:, :, :]).then_inc(p_row_stored[k], 16)
                for p in range(PER):
                    sp.wait_ge(p_col_kept[p], FROM + at + 1)
                sp.dma_start(
                    col_probs[bass.ds(b, 1), :, bass.ds(i * (SLOTS * CH) + k * CH, CH), :].rearrange(
                        "b g w h -> g (b w) h"), p_col_out[k][:, :, :]).then_inc(p_col_stored[k], 16)

            def blocks(b, first, last, chunks=None):
                def body(j):
                    i = j + first
                    for k in range(SLOTS):
                        load(b, i, k)
                        store_turned(b, i - 1, k)
                        if chunks is not None:
                            store_probs(chunks, j, k)
                loop(sp, last - first, body)

            for k in range(SLOTS):
                load(0, 0, k)
            blocks(0, 1, BODIES)

            def image(b, earlier):
                for k in range(SLOTS):
                    load(b, 0, k)
                    store_turned(b - 1, BODIES - 1, k)
                    if earlier:
                        store_probs(b - 2, HALF - 1, k)
                blocks(b, 1, HALF + 1)
                blocks(b, HALF + 1, BODIES, b - 1)
            if B > 1:
                image(1, False)
            if B > 2:
                loop(sp, B - 2, lambda c: image(c + 2, True))
            for k in range(SLOTS):
                store_turned(B - 1, BODIES - 1, k)
                if B > 1:
                    store_probs(B - 2, HALF - 1, k)

            def last_probs(i):
                for k in range(SLOTS):
                    store_probs(B - 1, i, k)
            loop(sp, HALF, last_probs)
            for k in range(SLOTS):
                sp.wait_ge(p_row_stored[k], FROM + B * HALF * 16)
                sp.wait_ge(p_col_stored[k], FROM + B * HALF * 16)
                sp.wait_ge(xt_stored[k], FROM + B * BODIES * 16)

        @block.tensor
        def _(pe):
            pe.wait_ge(consts_in, 4 * 16)

            def x_block(b, i, k, between=None):
                bank = k % 2
                used = (b * BODIES + i) * (SLOTS // 2) + k // 2
                pe.wait_ge(x_loaded[k], FROM + (b * BODIES + i + 1) * 16)

                def turn(g):
                    xt_bank, held = turned(b, i, k, g)
                    pe.wait_ge(xt_kept[xt_bank], FROM + held)
                    for t in range(KT):
                        mm = nc.tensor.transpose(ps[:, XT_BANK + xt_bank, t * P:(t + 1) * P],
                                                 x_in[k][:, t, g * P:(g + 1) * P], ident[:, :])
                    mm.then_inc(xt_turned[xt_bank], 1)

                def project(t):
                    return nc.tensor.matmul(ps[:, KQ_BANK + bank, 0:BP], wkq[:, t, :], x_in[k][:, t, :],
                                            start=(t == 0), stop=(t == KT - 1))
                for g in range(G - 1):
                    turn(g)
                pe.wait_ge(kq_kept[bank], FROM + used)
                for t in range(KT // 2):
                    project(t)
                if between:
                    between()
                turn(G - 1)
                for t in range(KT // 2, KT):
                    mm = project(t)
                mm.then_inc(kq_done[k], 1)

            def energies(b):
                for p in range(2):
                    pe.wait_ge(kq_kept[p], FROM + (b + 1) * (NB // 2))
                apart(pe)

                def body(i):
                    for p in range(2):
                        at = b * UP + i
                        pe.wait_ge(q_rows_laid[p], FROM + at + 1)
                        pe.wait_ge(e_row_kept[p], FROM + at)
                        for r in range(R):
                            mm = nc.tensor.matmul(ps[0:W, ROW_BANK + p, r * W:(r + 1) * W],
                                                  q_rows[p][:, r, :],
                                                  k_all[:, bass.ds(i * (2 * R) + p * R + r, 1), :].rearrange(
                                                      "c a w -> c (a w)"), start=True, stop=True)
                        mm.then_inc(e_row_mm[p], 1)
                        pe.wait_ge(q_cols_laid[p], FROM + at + 1)
                        pe.wait_ge(e_col_kept[p], FROM + at)
                        for r in range(R):
                            mm = nc.tensor.matmul(ps[0:H, COL_BANK + p, r * H:(r + 1) * H],
                                                  q_cols[p][:, r, :],
                                                  k_all[:, :, bass.ds(i * (2 * R) + p * R + r, 1)].rearrange(
                                                      "c h a -> c (h a)"), start=True, stop=True)
                        mm.then_inc(e_col_mm[p], 1)
                loop(pe, UP, body)

            def turn_stats(row, col):
                nc.tensor.transpose(ps[0:H, ROW_BANK, 0:W], row[:, :], ident[0:W, 0:W]).then_inc(stat_turned, 1)
                nc.tensor.transpose(ps[0:W, COL_BANK, 0:H], col[:, :], ident[0:H, 0:H]).then_inc(stat_turned, 1)

            def turn_maxima(b):
                pe.wait_ge(max_done, FROM + (b + 1) * NB * 2)
                turn_stats(max_row, max_col)

            def turn_sums(b):
                pe.wait_ge(sum_done, FROM + (b + 1) * NCH * 2)
                turn_stats(sum_row, sum_col)

            def turn_probs(b, i, k):
                at = b * NCH + i * SLOTS + k
                tile, _ = tile_of(b, i, k)
                pe.wait_ge(scaled_row, FROM + at + 1)
                for p in range(PER):
                    pe.wait_ge(p_row_kept[p], FROM + at)
                    for r in range(R):
                        mm = nc.tensor.transpose(
                            ps[0:W, ROW_BANK + p, r * W:(r + 1) * W],
                            p_row_in[tile][:, p * R + r, :], ident[0:W, 0:W])
                    mm.then_inc(p_row_turned[tile][p], 1)
                pe.wait_ge(scaled_col, FROM + at + 1)
                for p in range(PER):
                    pe.wait_ge(p_col_kept[p], FROM + at)
                    for r in range(R):
                        mm = nc.tensor.transpose(
                            ps[0:H, COL_BANK + p, r * H:(r + 1) * H],
                            p_col_in[tile][:, p * R + r, :], ident[0:H, 0:H])
                    mm.then_inc(p_col_turned[tile][p], 1)

            def drained(b):
                for p in range(PER):
                    pe.wait_ge(p_row_kept[p], FROM + (b + 1) * NCH)
                    pe.wait_ge(p_col_kept[p], FROM + (b + 1) * NCH)

            def first(i):
                for k in range(SLOTS):
                    x_block(0, i, k)
            loop(pe, BODIES, first)
            energies(0)
            turn_maxima(0)

            def image(c):
                b = c + 1
                def exps(i):
                    for k in range(SLOTS):
                        x_block(b, i, k)
                loop(pe, HALF, exps)
                turn_sums(c)
                pe.wait_ge(total_done, FROM + b * 2)
                apart(pe)

                def norms(i):
                    for k in range(SLOTS):
                        x_block(b, i + HALF, k, lambda: turn_probs(c, i, k))
                loop(pe, HALF, norms)
                drained(c)
                energies(b)
                turn_maxima(b)
            if B > 1:
                loop(pe, B - 1, image)
            turn_sums(B - 1)
            pe.wait_ge(total_done, FROM + B * 2)

            def last(i):
                for k in range(SLOTS):
                    turn_probs(B - 1, i, k)
            loop(pe, HALF, last)

        @block.scalar
        def _(act):
            act.wait_ge(consts_in, 4 * 16)

            def x_block(b, i, k, softmax=None):
                bank = k % 2
                act.wait_ge(xt_stored[k], FROM + (b * BODIES + i) * 16)
                for g in range(G):
                    xt_bank, used = turned(b, i, k, g)
                    if xt_bank == 0:
                        act.wait_ge(xt_turned[0], FROM + used + 1)
                        nc.scalar.activation(xt_out[k][:, g, :], ps[:, XT_BANK, 0:C],
                                             ACT.Copy).then_inc(xt_kept[0], 1)
                    if g == 1 and softmax:
                        softmax()
                act.wait_ge(kq_done[k], FROM + b * BODIES + i + 1)
                nc.scalar.activation(
                    kq_all[:, bass.ds(i * (SLOTS * R) + k * R, R), :].rearrange("c h w -> c (h w)"),
                    ps[:, KQ_BANK + bank, 0:BP], ACT.Identity,
                    bias=bkq[:, 0:1], scale=1.0).then_inc(kq_kept[bank], 1)

            def energies(b):
                def lay_rows(i, p):
                    act.wait_ge(e_row_mm[p], FROM + b * UP + i)
                    apart(act)
                    nc.scalar.activation(
                        q_rows[p][:, :, :].rearrange("c h w -> c (h w)"),
                        q_all[:, bass.ds(i * (2 * R) + p * R, R), :].rearrange("c h w -> c (h w)"),
                        ACT.Copy).then_inc(q_rows_laid[p], 1)

                def keep(i, p):
                    act.wait_ge(e_row_mm[p], FROM + b * UP + i + 1)
                    apart(act)
                    nc.scalar.activation(
                        e_row[:, bass.ds(i * (2 * R) + p * R, R), :].rearrange("w h v -> w (h v)"),
                        ps[0:W, ROW_BANK + p, 0:BP], ACT.Copy).then_inc(e_row_kept[p], 1)

                for p in range(2):
                    act.wait_ge(kq_kept[p], FROM + (b + 1) * (NB // 2))
                lay_rows(0, 0)

                def body(i):
                    lay_rows(i, 1)
                    keep(i, 0)
                    lay_rows(i + 1, 0)
                    keep(i, 1)
                loop(act, UP - 1, body)
                lay_rows(UP - 1, 1)
                keep(UP - 1, 0)
                keep(UP - 1, 1)

            def exps(b, chunk):
                at = b * NCH + chunk
                for j, e in enumerate((e_row, e_col)):
                    act.wait_ge(shifted, FROM + at * 2 + j + 1)
                    apart(act)
                    part = e[:, bass.ds(chunk * CH, CH), :].rearrange("a b c -> a (b c)")
                    nc.scalar.activation(part, part, ACT.Exp).then_inc(exp_done, 1)

            def keep_rows(b, i, k):
                tile, used = tile_of(b, i, k)
                act.wait_ge(p_row_stored[k], FROM + (b * HALF + i) * 16)
                for p in range(PER):
                    act.wait_ge(p_row_turned[tile][p], FROM + used + 1)
                    nc.scalar.activation(
                        p_row_out[k][:, p * R:(p + 1) * R, :].rearrange("v h w -> v (h w)"),
                        ps[0:W, ROW_BANK + p, 0:BP], ACT.Copy).then_inc(p_row_kept[p], 1)

            def first(i):
                for k in range(SLOTS):
                    x_block(0, i, k)
            loop(act, BODIES, first)
            energies(0)

            def image(c):
                b = c + 1
                for p in range(2):
                    act.wait_ge(e_row_mm[p], FROM + b * UP)
                    act.wait_ge(e_col_mm[p], FROM + b * UP)
                apart(act)

                def exp_body(i):
                    for k in range(SLOTS):
                        x_block(b, i, k, lambda: exps(c, i * SLOTS + k))
                loop(act, HALF, exp_body)

                def norm_body(i):
                    for k in range(SLOTS):
                        x_block(b, i + HALF, k, lambda: keep_rows(c, i, k))
                loop(act, HALF, norm_body)
                energies(b)
            if B > 1:
                loop(act, B - 1, image)

            def last_exps(i):
                for k in range(SLOTS):
                    exps(B - 1, i * SLOTS + k)
            loop(act, HALF, last_exps)

            def last_probs(i):
                for k in range(SLOTS):
                    keep_rows(B - 1, i, k)
            loop(act, HALF, last_probs)

        @block.vector
        def _(dve):
            dve.wait_ge(consts_in, 4 * 16)

            def x_block(b, i, k, softmax=lambda part: None):
                dve.wait_ge(xt_stored[k], FROM + (b * BODIES + i) * 16)
                for g in range(G):
                    xt_bank, used = turned(b, i, k, g)
                    if xt_bank == 1:
                        dve.wait_ge(xt_turned[1], FROM + used + 1)
                        nc.vector.tensor_copy(xt_out[k][:, g, :],
                                              ps[:, XT_BANK + 1, 0:C]).then_inc(xt_kept[1], 1)
                    if g > 0:
                        softmax(g - 1)

            def energies(b):
                def lay_cols(i, p):
                    dve.wait_ge(e_col_mm[p], FROM + b * UP + i)
                    nc.vector.tensor_copy(
                        q_cols[p][:, :, :],
                        q_all[:, :, bass.ds(i * (2 * R) + p * R, R)].rearrange("c h w -> c w h")
                    ).then_inc(q_cols_laid[p], 1)

                def keep(i, p):
                    at = b * UP + i
                    first = i * (2 * R) + p * R
                    dve.wait_ge(e_col_mm[p], FROM + at + 1)
                    part = e_col[:, bass.ds(first, R), :]
                    nc.vector.tensor_tensor(
                        part, ps[0:H, COL_BANK + p, 0:BP].rearrange("h (w g) -> h w g", w=R),
                        diag[:, :].unsqueeze(1).to_broadcast([H, R, H]), ALU.add).then_inc(e_col_kept[p], 1)
                    dve.wait_ge(e_row_kept[p], FROM + at + 1)
                    nc.vector.tensor_reduce(max_row[:, bass.ds(first, R)], e_row[:, bass.ds(first, R), :],
                                            AX_X, ALU.max).then_inc(max_done, 1)
                    dve.wait_ge(e_col_kept[p], FROM + at + 1)
                    nc.vector.tensor_reduce(max_col[:, bass.ds(first, R)], part,
                                            AX_X, ALU.max).then_inc(max_done, 1)

                for p in range(2):
                    dve.wait_ge(kq_kept[p], FROM + (b + 1) * (NB // 2))
                lay_cols(0, 0)

                def body(i):
                    lay_cols(i, 1)
                    keep(i, 0)
                    lay_cols(i + 1, 0)
                    keep(i, 1)
                loop(dve, UP - 1, body)
                lay_cols(UP - 1, 1)
                keep(UP - 1, 0)
                keep(UP - 1, 1)

            def join_maxima(b):
                dve.wait_ge(stat_turned, FROM + b * 4 + 2)
                nc.vector.tensor_tensor(max_col[:, :], ps[0:H, ROW_BANK, 0:W], max_col[:, :],
                                        ALU.max).then_inc(joint_done, 1)
                nc.vector.tensor_tensor(max_row[:, :], ps[0:W, COL_BANK, 0:H], max_row[:, :],
                                        ALU.max).then_inc(joint_done, 1)

            def join_sums(b):
                dve.wait_ge(stat_turned, FROM + b * 4 + 4)
                nc.vector.tensor_tensor(sum_col[:, :], ps[0:H, ROW_BANK, 0:W], sum_col[:, :],
                                        ALU.add).then_inc(total_done, 1)
                nc.vector.tensor_tensor(sum_row[:, :], ps[0:W, COL_BANK, 0:H], sum_row[:, :],
                                        ALU.add).then_inc(total_done, 1)
                dve.wait_ge(total_done, FROM + b * 2 + 2)
                nc.vector.reciprocal(sum_row[:, :], sum_row[:, :]).then_inc(inv_done, 1)
                nc.vector.reciprocal(sum_col[:, :], sum_col[:, :]).then_inc(inv_done, 1)
                dve.wait_ge(inv_done, FROM + b * 2 + 2)
                apart(dve)

            def sums(b, chunk, j):
                at = b * NCH + chunk
                e, total = ((e_row, sum_row), (e_col, sum_col))[j]
                dve.wait_ge(exp_done, FROM + at * 2 + j + 1)
                nc.vector.tensor_reduce(total[:, bass.ds(chunk * CH, CH)], e[:, bass.ds(chunk * CH, CH), :],
                                        AX_X, ALU.add).then_inc(sum_done, 1)

            def scale_cols(b, i, k):
                chunk = i * SLOTS + k
                tile, used = tile_of(b, i, k)
                for p in range(PER):
                    dve.wait_ge(p_col_turned[tile][p], FROM + used)
                nc.vector.tensor_tensor(
                    p_col_in[tile][:, :, :], e_col[:, bass.ds(chunk * CH, CH), :],
                    sum_col[:, bass.ds(chunk * CH, CH)].unsqueeze(2).to_broadcast([H, CH, H]),
                    ALU.mult).then_inc(scaled_col, 1)

            def keep_probs(b, i, k):
                tile, used = tile_of(b, i, k)
                dve.wait_ge(p_col_stored[k], FROM + (b * HALF + i) * 16)
                for p in range(PER):
                    dve.wait_ge(p_col_turned[tile][p], FROM + used + 1)
                    nc.vector.tensor_copy(
                        p_col_out[k][:, p * R:(p + 1) * R, :].rearrange("g w h -> g (w h)"),
                        ps[0:H, COL_BANK + p, 0:BP]).then_inc(p_col_kept[p], 1)

            def first(i):
                for k in range(SLOTS):
                    x_block(0, i, k)
            loop(dve, BODIES, first)
            energies(0)
            join_maxima(0)

            def image(c):
                b = c + 1

                def exp_body(i):
                    for k in range(SLOTS):
                        x_block(b, i, k, lambda j: sums(c, i * SLOTS + k, j))
                loop(dve, HALF, exp_body)
                join_sums(c)

                def norm_body(i):
                    for k in range(SLOTS):
                        scale_cols(c, i, k)
                        x_block(b, i + HALF, k, lambda j: keep_probs(c, i, k) if j == 0 else None)
                loop(dve, HALF, norm_body)
                energies(b)
                join_maxima(b)
            if B > 1:
                loop(dve, B - 1, image)

            def last_sums(i):
                for k in range(SLOTS):
                    for j in range(2):
                        sums(B - 1, i * SLOTS + k, j)
            loop(dve, HALF, last_sums)
            join_sums(B - 1)

            scale_cols(B - 1, 0, 0)

            def last_probs(i):
                for k in range(SLOTS):
                    scale_cols(B - 1, i + (k + 1) // SLOTS, (k + 1) % SLOTS)
                    keep_probs(B - 1, i, k)
            loop(dve, HALF - 1, last_probs)
            for k in range(SLOTS):
                if k + 1 < SLOTS:
                    scale_cols(B - 1, HALF - 1, k + 1)
                keep_probs(B - 1, HALF - 1, k)

        @block.gpsimd
        def _(pool):
            for s in counted:
                pool.sem_inc(s, FROM)

            def shift(b):
                pool.wait_ge(joint_done, FROM + (b + 1) * 2)
                apart(pool)

                def body(i):
                    for k in range(SLOTS):
                        chunk = i * SLOTS + k
                        for e, m in ((e_row, max_row), (e_col, max_col)):
                            part = e[:, bass.ds(chunk * CH, CH), :]
                            nc.gpsimd.tensor_tensor(
                                part, part, m[:, bass.ds(chunk * CH, CH)].unsqueeze(2).to_broadcast([H, CH, H]),
                                ALU.subtract).then_inc(shifted, 1)
                loop(pool, HALF, body)

            def scale_rows(b):
                pool.wait_ge(inv_done, FROM + (b + 1) * 2)
                apart(pool)

                def body(i):
                    for k in range(SLOTS):
                        chunk = i * SLOTS + k
                        tile, used = tile_of(b, i, k)
                        for p in range(PER):
                            pool.wait_ge(p_row_turned[tile][p], FROM + used)
                        nc.gpsimd.tensor_tensor(
                            p_row_in[tile][:, :, :], e_row[:, bass.ds(chunk * CH, CH), :],
                            sum_row[:, bass.ds(chunk * CH, CH)].unsqueeze(2).to_broadcast([W, CH, W]),
                            ALU.mult).then_inc(scaled_row, 1)
                loop(pool, HALF, body)

            def image(b):
                shift(b)
                scale_rows(b)
            loop(pool, B, image)


def attend_and_project(nc, x, wv_t, bv_d, gamma_d, ident_d, x_t, row_probs, col_probs, out):
    B, C, H, W = x.shape
    CT = C // P
    R = 3
    UP = R * W
    NU = H // R
    PAIRS = NU // 2
    SLOTS = 4
    FOURS = NU // SLOTS
    assert H == W and NU % SLOTS == 0 and (SLOTS - 2) * R * C <= 4 * CT * UP

    with ExitStack() as ctx:
        def sb(name, shape, dt=F32):
            return ctx.enter_context(nc.sbuf_tensor(name, shape, dt))

        counted = []

        def sem(name):
            counted.append(ctx.enter_context(nc.semaphore(name)))
            return counted[-1]

        y = sb("y", [P, CT, H * W])
        probs = [sb(f"probs{p}", [H, R, W]) for p in range(SLOTS)]
        x_res = [sb(f"x_res{p}", [P, CT, UP]) for p in range(2)]
        parts = sb("parts", [P, 4 * CT * UP], F32R)

        def part(j):
            return parts[:, j * CT * UP:(j + 1) * CT * UP].rearrange("p (t n) -> p t n", t=CT)
        y_hi = [part(0), part(1)]
        y_lo = [part(2), part(3)]
        xt_in = [sb(f"xt_in{p}", [H, R, C])[:, :, :] for p in range(2)]
        xt_in += [parts[0:H, j * R * C:(j + 1) * R * C].bitcast(F32).rearrange("s (r c) -> s r c", r=R)
                  for j in range(SLOTS - 2)]
        w_hi = sb("w_hi", [P, CT, C], F32R)
        w_lo = sb("w_lo", [P, CT, C], F32R)
        bv = sb("bv", [P, CT])
        gamma = sb("gamma", [P, 1])
        gamma_bv = sb("gamma_bv", [P, CT])
        ident = sb("ident_b", [H, H])
        att = [x_res[j // 2][0:H, :, :].rearrange("p t n -> p (t n)")[:, j % 2 * C:(j % 2 + 1) * C]
               for j in range(4)]

        ps = ctx.enter_context(nc.psum_tensor("ps_b", [P, 8, BANK], F32))

        passed = ctx.enter_context(nc.semaphore("passed"))
        params_in = ctx.enter_context(nc.semaphore("params_in"))
        ident_in = ctx.enter_context(nc.semaphore("ident_in"))
        w_split = ctx.enter_context(nc.semaphore("w_split"))
        scaled_bias = ctx.enter_context(nc.semaphore("scaled_bias"))
        cols_in = [sem(f"cols_in{k}") for k in range(SLOTS)]
        rows_in = [sem(f"rows_in{p}") for p in range(2)]
        res_in = [sem(f"res_in{p}") for p in range(2)]
        cols_mm = [sem(f"cols_mm{k}") for k in range(SLOTS)]
        att_kept = [sem(f"att_kept{j}") for j in range(4)]
        att_turned = [sem(f"att_turned{j}") for j in range(4)]
        cols_act = sem("cols_act")
        cols_dve = sem("cols_dve")
        rows_mm = sem("rows_mm")
        summed = sem("summed")
        hi_done = [sem(f"hi_done{p}") for p in range(2)]
        lo_done = [sem(f"lo_done{p}") for p in range(2)]
        proj_mm = [sem(f"proj_mm{p}") for p in range(2)]
        affine_done = sem("affine_done")
        final_done = sem("final_done")
        stored = sem("stored")

        w_raw = y[:, 0, 0:CT * C].rearrange("p (t o) -> p t o", t=CT)

        def apart(eng):
            eng.sem_inc(passed, 1)

        def loop(eng, n, body):
            with eng.Fori(0, n) as i:
                body(i)

        def column(at, k, r):
            c = k * R + r
            return c % 4, at * (SLOTS * R // 4) + c // 4

        def pipelined(eng, b, ahead, behind, free):
            ahead(b * FOURS, 0)
            free()
            apart(eng)

            def body(i):
                for k in range(SLOTS):
                    ahead(b * FOURS + i + (k + 1) // SLOTS, (k + 1) % SLOTS)
                    behind(b * FOURS + i, i * SLOTS + k, k)
            loop(eng, FOURS - 1, body)
            for k in range(SLOTS):
                if k + 1 < SLOTS:
                    ahead((b + 1) * FOURS - 1, k + 1)
                behind((b + 1) * FOURS - 1, NU - SLOTS + k, k)

        def pixels(t0, t1, first):
            return y[:, t0:t1, bass.ds(first * W, UP)]

        block = ctx.enter_context(nc.Block())

        @block.sync
        def _(sp):
            def load_cols(b, u, at, k):
                sp.wait_ge(cols_mm[k], FROM + at * R)
                sp.dma_start(xt_in[k], x_t[bass.ds(b, 1), :, bass.ds(u * R, R), :].rearrange(
                    "b h w c -> h (b w) c")).then_inc(cols_in[k], 16)
                sp.dma_start(probs[k][:, :, :], col_probs[bass.ds(b, 1), :, bass.ds(u * R, R), :].rearrange(
                    "b g w h -> g (b w) h")).then_inc(cols_in[k], 16)

            def load_rows(b, u, p):
                sp.dma_start(xt_in[p], x_t[bass.ds(b, 1), bass.ds(u * R, R), :, :].rearrange(
                    "b h w c -> w (b h) c")).then_inc(rows_in[p], 16)
                sp.dma_start(probs[p][:, :, :], row_probs[bass.ds(b, 1), :, bass.ds(u * R, R), :].rearrange(
                    "b v h w -> v (b h) w")).then_inc(rows_in[p], 16)

            def load_res(b, u, p):
                sp.dma_start(x_res[p][:, :, :], x[bass.ds(b, 1), :, bass.ds(u * R, R), :].rearrange(
                    "b (t p) h w -> p (b t) (h w)", p=P)).then_inc(res_in[p], 16)

            def store(b, u):
                sp.wait_ge(final_done, FROM + b * NU + u + 1)
                sp.dma_start(out[bass.ds(b, 1), :, bass.ds(u * R, R), :].rearrange(
                    "b (t p) h w -> p (b t) (h w)", p=P), pixels(0, CT, u * R)).then_inc(stored, 16)

            def image(b, more):
                def cols(i):
                    for k in range(SLOTS):
                        load_cols(b, i * SLOTS + k + SLOTS, b * FOURS + i + 1, k)
                loop(sp, FOURS - 1, cols)
                for k in range(2):
                    sp.wait_ge(cols_mm[k], FROM + (b + 1) * FOURS * R)
                    load_rows(b, k, k)
                for j in range(4):
                    sp.wait_ge(att_turned[j], FROM + (b + 1) * (NU * R // 4))
                for p in range(2):
                    load_res(b, p, p)
                sp.wait_ge(rows_mm, FROM + b * NU * 2 + 2)
                load_rows(b, 2, 0)

                def rows(i):
                    for p in range(2):
                        u = i * 2 + p
                        sp.wait_ge(rows_mm, FROM + (b * NU + u + 2) * 2)
                        load_rows(b, u + 3, 1 - p)
                        store(b, u)
                        load_res(b, u + 2, p)
                loop(sp, PAIRS - 2, rows)
                sp.wait_ge(rows_mm, FROM + (b * NU + NU - 2) * 2)
                load_rows(b, NU - 1, 1)
                store(b, NU - 4)
                load_res(b, NU - 2, 0)
                store(b, NU - 3)
                load_res(b, NU - 1, 1)
                if more:
                    for k in range(2):
                        sp.wait_ge(rows_mm, FROM + (b * NU + NU - 1 + k) * 2)
                        load_cols(b + 1, k, (b + 1) * FOURS, k)
                for p in range(2):
                    store(b, NU - 2 + p)
                if more:
                    for p in range(2):
                        sp.wait_ge(proj_mm[p], FROM + (b + 1) * PAIRS * CT)
                    for k in range(2, SLOTS):
                        load_cols(b + 1, k, (b + 1) * FOURS, k)
            load_cols(0, 0, 0, 0)
            sp.dma_start(ident[:, :], ident_d[0:H, 0:H]).then_inc(ident_in, 16)
            sp.dma_start(w_raw, wv_t.rearrange("(t p) o -> p t o", p=P)).then_inc(params_in, 16)
            sp.dma_start(bv[:, :], bv_d).then_inc(params_in, 16)
            sp.dma_start(gamma[:, :], gamma_d).then_inc(params_in, 16)
            for k in range(1, SLOTS):
                load_cols(0, k, 0, k)
            if B > 1:
                loop(sp, B - 1, lambda b: image(b, True))
            image(B - 1, False)
            sp.wait_ge(stored, FROM + B * NU * 16)

        @block.tensor
        def _(pe):
            def attend_cols(at, k):
                pe.wait_ge(cols_in[k], FROM + (at + 1) * 32)
                for r in range(R):
                    bank, used = column(at, k, r)
                    pe.wait_ge(att_kept[bank], FROM + used)
                    nc.tensor.matmul(ps[0:H, bank, 0:C], probs[k][:, r, :], xt_in[k][:, r, :],
                                     start=True, stop=True).then_inc(cols_mm[k], 1)

            def turn_cols(at, u, k):
                unit = at * SLOTS + k
                pe.wait_ge(cols_act, FROM + unit)
                pe.wait_ge(cols_dve, FROM + unit)
                for r in range(R):
                    j, used = column(at, k, r)
                    pe.wait_ge(att_kept[j], FROM + used + 1)
                    for t in range(CT):
                        mm = nc.tensor.transpose(ps[:, CT + t, r * H:(r + 1) * H],
                                                 att[j][:, t * P:(t + 1) * P], ident[:, :])
                    mm.then_inc(att_turned[j], 1)

            def attend_rows(b, u, at, p):
                pe.wait_ge(rows_in[p], FROM + (at + 1) * 32)
                pe.wait_ge(summed, FROM + (b * NU + u) * 2)
                for t in range(CT):
                    for r in range(R):
                        mm = nc.tensor.matmul(ps[:, t, r * W:(r + 1) * W],
                                              xt_in[p][:, r, t * P:(t + 1) * P], probs[p][:, r, :],
                                              start=True, stop=True)
                    if t % 2:
                        mm.then_inc(rows_mm, 1)

            def project(b, u, at, p):
                pe.wait_ge(hi_done[p], FROM + (at + 1) * 2)
                pe.wait_ge(lo_done[p], FROM + (at + 1) * 2)
                for m in range(CT):
                    pe.wait_ge(affine_done, FROM + (b * NU + u) * CT)
                    cols = slice(m * P, (m + 1) * P)
                    n = 0
                    for t in range(CT):
                        for w, v in ((w_hi, y_hi), (w_hi, y_lo), (w_lo, y_hi)):
                            mm = nc.tensor.matmul(ps[:, CT + m, 0:UP], w[:, t, cols], v[p][:, t, :],
                                                  start=(n == 0), stop=(n == 3 * CT - 1))
                            n += 1
                    mm.then_inc(proj_mm[p], 1)

            pe.wait_ge(ident_in, 16)

            def image(b):
                at0 = b * PAIRS
                pe.wait_ge(summed, FROM + b * NU * 2)
                pipelined(pe, b, attend_cols, turn_cols,
                          lambda: pe.wait_ge(affine_done, FROM + b * NU * CT))
                for j in range(4):
                    pe.wait_ge(att_kept[j], FROM + (b + 1) * (NU * R // 4))
                pe.wait_ge(cols_act, FROM + (b + 1) * NU)
                pe.wait_ge(cols_dve, FROM + (b + 1) * NU)
                attend_rows(b, 0, at0, 0)
                pe.wait_ge(w_split, 2)

                def rows(i):
                    attend_rows(b, i * 2 + 1, at0 + i, 1)
                    project(b, i * 2, at0 + i, 0)
                    attend_rows(b, i * 2 + 2, at0 + i + 1, 0)
                    project(b, i * 2 + 1, at0 + i, 1)
                loop(pe, PAIRS - 1, rows)
                attend_rows(b, NU - 1, at0 + PAIRS - 1, 1)
                project(b, NU - 2, at0 + PAIRS - 1, 0)
                project(b, NU - 1, at0 + PAIRS - 1, 1)
            loop(pe, B, image)

        @block.scalar
        def _(act):
            act.wait_ge(params_in, 48)
            nc.scalar.activation(w_hi[:, :, :], w_raw, ACT.Copy).then_inc(w_split, 1)
            act.wait_ge(scaled_bias, 1)
            act.wait_ge(w_split, 2)

            def keep_att(at, k):
                for r in range(R):
                    j, used = column(at, k, r)
                    if j % 2 == 0:
                        act.wait_ge(cols_mm[k], FROM + at * R + r + 1)
                        act.wait_ge(att_turned[j], FROM + used)
                        nc.scalar.activation(att[j], ps[0:H, j, 0:C], ACT.Copy).then_inc(att_kept[j], 1)

            def keep_cols(at, u, k):
                j, used = column(at, k, R - 1)
                act.wait_ge(att_turned[j], FROM + used + 1)
                for t in range(0, CT, 2):
                    copy = nc.scalar.activation(
                        y[:, t, :].rearrange("p (h w) -> p h w", h=H)[:, :, bass.ds(u * R, R)],
                        ps[:, CT + t, 0:UP].rearrange("p (w h) -> p h w", w=R), ACT.Copy)
                copy.then_inc(cols_act, 1)

            def high(b, u, at, p):
                act.wait_ge(proj_mm[p], FROM + at * CT)
                for j in range(2):
                    act.wait_ge(summed, FROM + (b * NU + u) * 2 + j + 1)
                    nc.scalar.activation(y_hi[p][:, 2 * j:2 * j + 2, :], pixels(2 * j, 2 * j + 2, u * R),
                                         ACT.Copy).then_inc(hi_done[p], 1)

            def affine(b, u, at, p):
                act.wait_ge(lo_done[p], FROM + (at + 1) * 2)
                act.wait_ge(hi_done[p], FROM + (at + 1) * 2)
                for m in range(CT):
                    act.wait_ge(proj_mm[p], FROM + at * CT + m + 1)
                    apart(act)
                    nc.scalar.activation(pixels(m, m + 1, u * R).rearrange("p a n -> p (a n)"), ps[:, CT + m, 0:UP],
                                         ACT.Identity, bias=gamma_bv[:, m:m + 1],
                                         scale=gamma[:, 0:1]).then_inc(affine_done, 1)

            def image(b):
                at0 = b * PAIRS
                act.wait_ge(final_done, FROM + b * NU)
                pipelined(act, b, keep_att, keep_cols,
                          lambda: act.wait_ge(stored, FROM + b * NU * 16))
                high(b, 0, at0, 0)

                def rows(i):
                    high(b, i * 2 + 1, at0 + i, 1)
                    affine(b, i * 2, at0 + i, 0)
                    high(b, i * 2 + 2, at0 + i + 1, 0)
                    affine(b, i * 2 + 1, at0 + i, 1)
                loop(act, PAIRS - 1, rows)
                high(b, NU - 1, at0 + PAIRS - 1, 1)
                affine(b, NU - 2, at0 + PAIRS - 1, 0)
                affine(b, NU - 1, at0 + PAIRS - 1, 1)
            loop(act, B, image)

        @block.vector
        def _(dve):
            dve.wait_ge(params_in, 48)
            nc.vector.tensor_scalar(gamma_bv[:, :], bv[:, :], gamma[:, 0:1], None,
                                    ALU.mult).then_inc(scaled_bias, 1)
            dve.wait_ge(w_split, 1)
            nc.vector.tensor_tensor(w_lo[:, :, :], w_raw, w_hi[:, :, :].bitcast(F32),
                                    ALU.subtract).then_inc(w_split, 1)
            dve.wait_ge(w_split, 2)

            def keep_att(at, k):
                for r in range(R):
                    j, used = column(at, k, r)
                    if j % 2:
                        dve.wait_ge(cols_mm[k], FROM + at * R + r + 1)
                        dve.wait_ge(att_turned[j], FROM + used)
                        nc.vector.tensor_copy(att[j], ps[0:H, j, 0:C]).then_inc(att_kept[j], 1)

            def keep_cols(at, u, k):
                j, used = column(at, k, R - 1)
                dve.wait_ge(att_turned[j], FROM + used + 1)
                for t in range(1, CT, 2):
                    copy = nc.vector.tensor_copy(
                        y[:, t, :].rearrange("p (h w) -> p h w", h=H)[:, :, bass.ds(u * R, R)],
                        ps[:, CT + t, 0:UP].rearrange("p (w h) -> p h w", w=R))
                copy.then_inc(cols_dve, 1)

            def add_rows(b, u, at, p):
                for j in range(2):
                    dve.wait_ge(rows_mm, FROM + (b * NU + u) * 2 + j + 1)
                    part = pixels(2 * j, 2 * j + 2, u * R)
                    nc.vector.tensor_tensor(part, ps[:, 2 * j:2 * j + 2, 0:UP], part,
                                            ALU.add).then_inc(summed, 1)
                dve.wait_ge(proj_mm[p], FROM + at * CT)
                for j in range(2):
                    dve.wait_ge(summed, FROM + (b * NU + u) * 2 + j + 1)
                    dve.wait_ge(hi_done[p], FROM + at * 2 + j + 1)
                    nc.vector.tensor_tensor(y_lo[p][:, 2 * j:2 * j + 2, :], pixels(2 * j, 2 * j + 2, u * R),
                                            y_hi[p][:, 2 * j:2 * j + 2, :].bitcast(F32),
                                            ALU.subtract).then_inc(lo_done[p], 1)

            def image(b):
                at0 = b * PAIRS
                dve.wait_ge(final_done, FROM + b * NU)
                pipelined(dve, b, keep_att, keep_cols,
                          lambda: dve.wait_ge(stored, FROM + b * NU * 16))
                dve.wait_ge(cols_act, FROM + (b + 1) * NU)
                dve.wait_ge(cols_dve, FROM + (b + 1) * NU)
                apart(dve)

                def rows(i):
                    for p in range(2):
                        add_rows(b, i * 2 + p, at0 + i, p)
                loop(dve, PAIRS, rows)
            loop(dve, B, image)

        @block.gpsimd
        def _(pool):
            for s in counted:
                pool.sem_inc(s, FROM)

            def image(b):
                def rows(i):
                    for p in range(2):
                        u = i * 2 + p
                        pool.wait_ge(res_in[p], FROM + (b * PAIRS + i + 1) * 16)
                        pool.wait_ge(affine_done, FROM + (b * NU + u + 1) * CT)
                        part = pixels(0, CT, u * R)
                        nc.gpsimd.tensor_tensor(part, part, x_res[p][:, :, :], ALU.add).then_inc(final_done, 1)
                loop(pool, PAIRS, rows)
            loop(pool, B, image)


def kernel(x, L0_conv_Wq, L0_conv_bq, L0_conv_Wk, L0_conv_bk, L0_conv_Wv, L0_conv_bv, L0_conv_gamma):
    import concourse.bacc as bacc
    from concourse.bass_utils import run_bass_kernel_spmd

    x = np.ascontiguousarray(x)
    wq, wk, wv = np.asarray(L0_conv_Wq), np.asarray(L0_conv_Wk), np.asarray(L0_conv_Wv)
    side = x.shape[2]
    arrays = {
        "x": x,
        "wkq_t": np.ascontiguousarray(np.concatenate([wk, wq]).T),
        "bias_kq": np.concatenate([np.asarray(L0_conv_bk), np.asarray(L0_conv_bq)]).reshape(P, 1),
        "wv_t": np.ascontiguousarray(wv.T),
        "bv": np.ascontiguousarray(np.asarray(L0_conv_bv).reshape(-1, P).T),
        "gamma": np.ascontiguousarray(np.tile(np.asarray(L0_conv_gamma), P).reshape(P, 1)),
        "ident": np.eye(P, dtype=np.float32),
        "diag": np.where(np.eye(side, dtype=bool), np.float32(MASKED), np.float32(0)).astype(np.float32),
    }
    nc = bacc.Bacc("TRN2", target_bir_lowering=False, num_devices=1)
    args = [nc.dram_tensor(f"{n}_dram", a.shape, F32, kind="ExternalInput").ap() for n, a in arrays.items()]
    out = nc.dram_tensor("out_dram", x.shape, F32, kind="ExternalOutput").ap()
    build_program(nc, *args, out)
    r = run_bass_kernel_spmd(nc, [{f"{n}_dram": a for n, a in arrays.items()}], core_ids=[0])
    return r.results[0]["out_dram"]
```
